# Optimizing a Trainium2 kernel written in Bass

```python
import numpy as np
import jax
import jax.numpy as jnp

def _softmax(x, axis=-1):
    return jax.nn.softmax(x, axis=axis)

def _gelu(x):
    return jax.nn.gelu(x, approximate=True)

def _silu(x):
    return jax.nn.silu(x)

def _sigmoid(x):
    return jax.nn.sigmoid(x)

def _layernorm(x, axis=-1, eps=1e-05):
    m = jnp.mean(x, axis=axis, keepdims=True)
    v = jnp.var(x, axis=axis, keepdims=True)
    return (x - m) / jnp.sqrt(v + eps)

def _scatter_add(tgt, idx, src, axis=0):
    return tgt.at[idx].add(src)

def _segment_sum(src, seg, n):
    return jax.ops.segment_sum(src, seg, n)
kernel_name = 'mk_gnn_preln_d1_gnn_r32_bc9a25'

def setup_inputs(seed: int=0):
    np.random.seed(seed)
    _w = jnp.asarray

    def _rec_inputs():
        import jax
        import jax.numpy as jnp
        _gk = jax.random.key(seed)
        x = -0.0005121 + 1.001 * jax.random.normal(jax.random.fold_in(_gk, 1), (3125, 64), jnp.float32)
        _s = jax.random.randint(jax.random.fold_in(_gk, 2), (25000,), 0, 3125, jnp.int32)
        _d = jax.random.randint(jax.random.fold_in(_gk, 3), (25000,), 0, 3125, jnp.int32)
        _loop = jnp.arange(3125, dtype=jnp.int32)
        src = jnp.concatenate([_s, _d, _loop])
        dst = jnp.concatenate([_d, _s, _loop])
        _o = jnp.argsort(dst, stable=True)
        src = src[_o]
        dst = dst[_o]
        edge_attr_64 = 0.000189758 + 1.00013 * jax.random.normal(jax.random.fold_in(_gk, 12), (53125, 64), jnp.float32)
        return (x, src, dst, edge_attr_64)
    x, src, dst, edge_attr_64 = _rec_inputs()

    def _L0_gnn_setup():
        import jax, jax.numpy as jnp
        import numpy as np
        N_NODES = 50000
        N_EDGES = 25000
        IN_NODE = 64
        IN_EDGE = 64
        HIDDEN = 128
        OUT_NODE = 64

        def _linear_params(key, fan_in, fan_out):
            k1, k2 = jax.random.split(key)
            bound = 1.0 / np.sqrt(fan_in)
            W = jax.random.uniform(k1, (fan_out, fan_in), jnp.float32, -bound, bound)
            b = jax.random.uniform(k2, (fan_out,), jnp.float32, -bound, bound)
            return (W, b)
        key = jax.random.key(seed)
        ks = jax.random.split(key, 10)
        src_node_features = jax.random.normal(ks[0], (N_NODES, IN_NODE), jnp.float32)
        edge_index = jax.random.randint(ks[1], (2, N_EDGES), 0, N_NODES, dtype=jnp.int32).astype(jnp.int64)
        edge_attr = jax.random.normal(ks[2], (N_EDGES, IN_EDGE), jnp.float32)
        u = jax.random.normal(ks[3], (1, 16), jnp.float32)
        batch = jnp.zeros((N_NODES,), jnp.int64)
        W1a, b1a = _linear_params(ks[4], IN_NODE + IN_EDGE, HIDDEN)
        W1b, b1b = _linear_params(ks[5], HIDDEN, OUT_NODE)
        W2a, b2a = _linear_params(ks[6], IN_NODE + OUT_NODE, HIDDEN)
        W2b, b2b = _linear_params(ks[7], HIDDEN, OUT_NODE)
        Wr, br = _linear_params(ks[8], OUT_NODE + IN_NODE, OUT_NODE)
        return {'src_node_features': src_node_features, 'edge_index': edge_index, 'edge_attr': edge_attr, 'u': u, 'batch': batch, 'W1a': W1a, 'b1a': b1a, 'W1b': W1b, 'b1b': b1b, 'W2a': W2a, 'b2a': b2a, 'W2b': W2b, 'b2b': b2b, 'Wr': Wr, 'br': br}
    _L0_gnn_all = _L0_gnn_setup()
    _L0_gnn_in = {k: v for k, v in _L0_gnn_all.items() if k in ('u', 'W1a', 'b1a', 'W1b', 'b1b', 'W2a', 'b2a', 'W2b', 'b2b', 'Wr', 'br')}
    del _L0_gnn_all
    return {'x': x, 'src': src, 'dst': dst, 'edge_attr_64': edge_attr_64, 'L0_gnn_u': _L0_gnn_in['u'], 'L0_gnn_W1a': _L0_gnn_in['W1a'], 'L0_gnn_b1a': _L0_gnn_in['b1a'], 'L0_gnn_W1b': _L0_gnn_in['W1b'], 'L0_gnn_b1b': _L0_gnn_in['b1b'], 'L0_gnn_W2a': _L0_gnn_in['W2a'], 'L0_gnn_b2a': _L0_gnn_in['b2a'], 'L0_gnn_W2b': _L0_gnn_in['W2b'], 'L0_gnn_b2b': _L0_gnn_in['b2b'], 'L0_gnn_Wr': _L0_gnn_in['Wr'], 'L0_gnn_br': _L0_gnn_in['br']}

def reference(x, src, dst, edge_attr_64, L0_gnn_u, L0_gnn_W1a, L0_gnn_b1a, L0_gnn_W1b, L0_gnn_b1b, L0_gnn_W2a, L0_gnn_b2a, L0_gnn_W2b, L0_gnn_b2b, L0_gnn_Wr, L0_gnn_br):
    import jax
    import jax.numpy as jnp

    def _L0_gnn_ref(src_node_features, edge_index, edge_attr, u, batch, W1a, b1a, W1b, b1b, W2a, b2a, W2b, b2b, Wr, br):
        import jax, jax.numpy as jnp
        import numpy as np
        N_NODES = 50000
        N_EDGES = 25000
        IN_NODE = 64
        IN_EDGE = 64
        HIDDEN = 128
        OUT_NODE = 64

        def _linear_params(key, fan_in, fan_out):
            k1, k2 = jax.random.split(key)
            bound = 1.0 / np.sqrt(fan_in)
            W = jax.random.uniform(k1, (fan_out, fan_in), jnp.float32, -bound, bound)
            b = jax.random.uniform(k2, (fan_out,), jnp.float32, -bound, bound)
            return (W, b)
        n_nodes = src_node_features.shape[0]
        row, col = (edge_index[0], edge_index[1])
        msg = jnp.concatenate([src_node_features[col], edge_attr], axis=1)
        h = jax.nn.relu(msg @ W1a.T + b1a)
        h = h @ W1b.T + b1b
        sums = jax.ops.segment_sum(h, row, num_segments=n_nodes)
        counts = jax.ops.segment_sum(jnp.ones((h.shape[0],), h.dtype), row, num_segments=n_nodes)
        agg = sums / jnp.maximum(counts, 1.0)[:, None]
        z = jnp.concatenate([src_node_features, agg], axis=1)
        z = jax.nn.relu(z @ W2a.T + b2a)
        z = z @ W2b.T + b2b
        out = jnp.concatenate([z, src_node_features], axis=1) @ Wr.T + br
        return out
    edge_index = jnp.stack([src, dst])
    batch0 = jnp.zeros((3125,), jnp.int32)
    h = jnp.maximum(_layernorm(x, axis=-1), 0.0)
    x = x + _L0_gnn_ref(h, edge_index, edge_attr_64, L0_gnn_u, batch0, L0_gnn_W1a, L0_gnn_b1a, L0_gnn_W1b, L0_gnn_b1b, L0_gnn_W2a, L0_gnn_b2a, L0_gnn_W2b, L0_gnn_b2b, L0_gnn_Wr, L0_gnn_br)
    return x

_drawn_inputs = setup_inputs


def setup_inputs(seed=0):
    import zlib

    import numpy as np

    out = dict(_drawn_inputs(seed))
    spreads = {}
    factors = {'edge_attr_64': 8.0,
     'L0_gnn_W1a': 8.0,
     'L0_gnn_b1a': 31.231,
     'L0_gnn_W1b': 8.0,
     'L0_gnn_b1b': 60.644,
     'L0_gnn_b2a': 28.118,
     'L0_gnn_b2b': 11.325,
     'L0_gnn_br': 4.42}
    for name, (base, spread) in spreads.items():
        noise = np.random.default_rng([zlib.crc32(name.encode()), seed]).standard_normal(out[name].shape)
        drawn = base * np.exp(spread * noise) if base else spread * noise
        out[name] = jnp.asarray(drawn.astype(out[name].dtype))
    for name, factor in factors.items():
        out[name] = (out[name] * factor).astype(out[name].dtype)
    return out
```

```python
import concourse.bass as bass
from concourse import mybir
from contextlib import ExitStack


def gnn_layer(nc, x, src, dst, edge_attr, W1a, b1a, W1b, b1b, W2a, b2a, W2b, b2b, Wr, br, out):
    f32, i32 = mybir.dt.float32, mybir.dt.int32
    ALU, ACT, AX = mybir.AluOpType, mybir.ActivationFunctionType, mybir.AxisListType

    N, D = x.shape
    E = src.shape[0]
    HID = W1a.shape[0]
    NB = 25
    BN = N // NB
    K = 8
    GE = 128 * K
    NG = (E + GE - 1) // GE
    LAST = E - (NG - 1) * GE
    LP, LR = LAST // K, LAST % K
    MW = D + 1
    PER_BANK = 7
    NBANK = (NB + PER_BANK - 1) // PER_BANK
    EPS = 1e-5

    with ExitStack() as ctx:
        def sb(name, shape, dt=f32):
            return ctx.enter_context(nc.sbuf_tensor(name, shape, dt))

        def ps(name, shape, dt=f32):
            return ctx.enter_context(nc.psum_tensor(name, shape, dt))

        def sem(name):
            return ctx.enter_context(nc.semaphore(name))

        ident = sb("ident", [128, 128])
        ones_row = sb("ones_row", [1, 128])
        node_row = sb("node_row", [128, NB * BN])
        rec_mark = sb("rec_mark", [128, 1])
        w1a_in = sb("w1a_in", [HID, 2 * D])
        w1b_in = sb("w1b_in", [D, HID])
        w2a_in = sb("w2a_in", [HID, 2 * D])
        w2b_in = sb("w2b_in", [D, HID])
        wr_in = sb("wr_in", [D, 2 * D])
        w1aT = sb("w1aT", [2 * D, HID])
        weT = sb("weT", [D, HID])
        w1bT = sb("w1bT", [HID, D])
        w2aT = sb("w2aT", [2 * D, HID])
        w2bT = sb("w2bT", [HID, D])
        wrzT = sb("wrzT", [D, D])
        wrhT = sb("wrhT", [D, D])
        b1a_row = sb("b1a_row", [1, HID])
        b1b_row = sb("b1b_row", [1, D])
        br_row = sb("br_row", [1, D])
        b1b_all = sb("b1b_all", [128, D])
        br_all = sb("br_all", [128, D])
        b2a_col = sb("b2a_col", [HID, 1])
        b2b_col = sb("b2b_col", [D, 1])

        xs = sb("xs", [BN, NB, D])
        h_agg = sb("h_agg", [BN, NB, 2 * D])
        xc = sb("xc", [BN, NB, D])
        xsq = sb("xsq", [BN, NB, D])
        stat = sb("stat", [BN, 4, NB])
        hT = sb("hT", [D, NB, BN])
        proj = sb("proj", [BN, 2, HID])
        sums = sb("sums", [BN, NB, MW])
        cnt = sb("cnt", [BN, 3, NB])
        catT = sb("catT", [2 * D, 2, BN])
        z1T = sb("z1T", [HID, BN])
        zT = sb("zT", [D, BN])
        ot = sb("ot", [BN, NB, D])
        proj_dram = nc.dram_tensor("proj_dram", (N, HID), f32, kind="Internal").ap()

        idx_i = sb("idx_i", [NG, 2, GE], i32)
        idx_f = sb("idx_f", [NG, 2, GE])
        srcL = sb("srcL", [128, NG, K])
        dstL = sb("dstL", [128, NG, K], i32)
        srcq = sb("srcq", [128, NG, K])
        mark = sb("mark", [128, NG, K])
        ea = sb("ea", [128, 2, K, D])
        dst_now = sb("dst_now", [128, K], i32)
        pg = sb("pg", [128, K, HID])
        eaT = sb("eaT", [D, 128])
        rT = sb("rT", [HID, 128])
        msg = sb("msg", [128, MW])
        onehot = sb("onehot", [128, NB, BN])

        acc = ps("acc", [128, NBANK, 512])
        pA = ps("pA", [128, 512])
        pB = ps("pB", [128, 512])
        pC = ps("pC", [128, 512])
        pD = ps("pD", [128, 512])

        def acc_of(b):
            c = (b % PER_BANK) * MW
            return acc[0:BN, b // PER_BANK, c:c + MW]

        s_w = sem("weights_loaded")
        s_x = sem("x_loaded")
        s_idx = sem("indices_loaded")
        s_pad = sem("pads_set")
        s_id = sem("identity_made")
        s_iota = sem("node_row_made")
        s_v = sem("vector_step")
        s_a = sem("scalar_step")
        s_tr = sem("pe_transposed")
        s_ev = sem("vector_evacuated")
        s_proj = sem("projection_made")
        s_pe_ev = sem("projection_evacuated")
        s_pst = [sem("projection_stored_0"), sem("projection_stored_1")]
        s_ea = [sem("edges_loaded_0"), sem("edges_loaded_1")]
        s_stage = sem("indices_staged")
        s_g = [sem(f"rows_gathered_{k}") for k in range(K)]
        s_eT = sem("edges_transposed")
        s_eTe = sem("edges_T_evacuated")
        s_h = sem("hidden_made")
        s_r = sem("hidden_relu")
        s_m = sem("message_made")
        s_me = sem("message_evacuated")
        s_used = sem("tile_accumulated")
        s_sum = sem("sums_evacuated")
        s_cat = sem("mean_made")
        s_ct = sem("cat_transposed")
        s_cte = sem("cat_evacuated")
        s_z1 = sem("z1_made")
        s_z1e = sem("z1_relu")
        s_z = sem("z_made")
        s_ze = sem("z_biased")
        s_o = sem("out_made")
        s_oe = sem("out_added")
        s_out = sem("out_stored")
        s_gate = sem("passed")
        NW = 12

        block = ctx.enter_context(nc.Block())

        @block.sync
        def _(sp):
            sp.wait_ge(s_pad, 1)
            for n, a in enumerate((src, dst)):
                sp.dma_start(idx_i[0:NG - 1, n, :], a[0:(NG - 1) * GE].rearrange("(g e) -> g e", e=GE)).then_inc(s_idx, 16)
                sp.dma_start(idx_i[NG - 1:NG, n, 0:LAST], a[(NG - 1) * GE:E].rearrange("(g e) -> g e", g=1)).then_inc(s_idx, 16)
            sp.dma_start(xs[:], x.rearrange("(b p) f -> p b f", p=BN)).then_inc(s_x, 16)
            for t, a in ((w1a_in, W1a), (w1b_in, W1b), (w2a_in, W2a), (w2b_in, W2b), (wr_in, Wr)):
                sp.dma_start(t[:], a).then_inc(s_w, 16)
            for t, a in ((b1a_row, b1a), (b1b_row, b1b), (br_row, br)):
                sp.dma_start(t[:], a.rearrange("(o n) -> o n", o=1)).then_inc(s_w, 16)
            for t, a in ((b1b_all, b1b), (br_all, br)):
                sp.dma_start(t[:], a.rearrange("(o n) -> o n", o=1).to_broadcast((128, D))).then_inc(s_w, 16)
            for t, a in ((b2a_col, b2a), (b2b_col, b2b)):
                sp.dma_start(t[:], a.rearrange("(n o) -> n o", o=1)).then_inc(s_w, 16)
            for b in range(NB):
                sp.wait_ge(s_pe_ev, b + 1)
                sp.dma_start(proj_dram[b * BN:(b + 1) * BN, :], proj[:, b % 2, :]).then_inc(s_pst[b % 2], 16)
            for g in range(2):
                sp.dma_start(ea[:, g, :, :], edge_attr[g * GE:(g + 1) * GE, :].rearrange("(p k) f -> p k f", k=K)).then_inc(s_ea[g], 16)
            def load(g, slot):
                sp.wait_ge(s_used, g * K - K)
                sp.dma_start(ea[:, slot, :, :], edge_attr[bass.ds(g * GE, GE), :].rearrange("(p k) f -> p k f", k=K)).then_inc(s_ea[slot], 16)

            with sp.Fori(1, NG // 2 - 1) as i:
                load(i * 2, 0)
                load(i * 2 + 1, 1)
            load(NG - 2, 0)
            sp.wait_ge(s_used, (NG - 2) * K)
            g0 = (NG - 1) * GE
            sp.dma_start(ea[0:LP, 1, :, :], edge_attr[g0:g0 + LP * K, :].rearrange("(p k) f -> p k f", k=K)).then_inc(s_ea[1], 16)
            sp.dma_start(ea[LP:LP + 1, 1, 0:LR, :], edge_attr[g0 + LP * K:E, :].rearrange("(p k) f -> p k f", k=LR)).then_inc(s_ea[1], 16)
            sp.wait_ge(s_oe, NB)
            sp.dma_start(out.rearrange("(b p) f -> p b f", p=BN), ot[:]).then_inc(s_out, 16)
            sp.wait_ge(s_out, 16)

        @block.gpsimd
        def _(pool):
            nc.gpsimd.memset(idx_i[:, 0, :], NB * BN)
            nc.gpsimd.memset(idx_i[:, 1, :], N - 1).then_inc(s_pad, 1)
            nc.gpsimd.memset(ident[:], 0.0).then_inc(s_id, 1)
            pool.wait_ge(s_id, 1)
            nc.gpsimd.affine_select(out=ident[:], in_=ident[:], compare_op=ALU.not_equal, fill=1.0, base=0,
                                    pattern=[[-1, 128]], channel_multiplier=1).then_inc(s_id, 1)
            nc.gpsimd.iota(node_row[:], pattern=[[1, NB * BN]], base=0, channel_multiplier=0,
                           allow_small_or_imprecise_dtypes=True).then_inc(s_iota, 1)
            nc.gpsimd.iota(rec_mark[:], pattern=[[0, 1]], base=1, channel_multiplier=1,
                           allow_small_or_imprecise_dtypes=True).then_inc(s_iota, 1)
            nc.gpsimd.memset(ones_row[:], 1.0).then_inc(s_iota, 1)
            pool.wait_ge(s_pst[0], 16 * ((NB + 1) // 2))
            pool.wait_ge(s_pst[1], 16 * (NB // 2))
            with pool.Fori(0, NG) as g:
                pool.wait_ge(s_stage, g + 1)
                pool.sem_inc(s_gate, 1)
                for k in range(K):
                    pool.indirect_dma_start(out=pg[:, k, :], out_offset=None, in_=proj_dram,
                                            in_offset=bass.IndirectOffsetOnAxis(ap=dst_now[:, k:k + 1], axis=0)
                                            ).then_inc(s_g[k], 16)

        @block.vector
        def _(dve):
            done = [0]

            def link(ins):
                done[0] += 1
                ins.then_inc(s_v, 1)
                dve.wait_ge(s_v, done[0])

            V = nc.vector
            dve.wait_ge(s_x, 16)
            bc = (BN, NB, D)
            link(V.tensor_reduce(stat[:, 0, :], xs[:], axis=AX.X, op=ALU.add))
            link(V.tensor_scalar(stat[:, 0, :], stat[:, 0, :], 1.0 / D, None, ALU.mult))
            link(V.tensor_tensor(xc[:], xs[:], stat[:, 0, :].unsqueeze(2).to_broadcast(bc), ALU.subtract))
            link(V.tensor_tensor(xsq[:], xc[:], xc[:], ALU.mult))
            link(V.tensor_reduce(stat[:, 1, :], xsq[:], axis=AX.X, op=ALU.add))
            link(V.tensor_scalar(stat[:, 1, :], stat[:, 1, :], 1.0 / D, EPS, ALU.mult, ALU.add))
            dve.wait_ge(s_a, 1)
            link(V.reciprocal(stat[:, 3, :], stat[:, 2, :]))
            link(V.tensor_tensor(xc[:], xc[:], stat[:, 3, :].unsqueeze(2).to_broadcast(bc), ALU.mult))
            link(V.tensor_scalar(h_agg[:, :, 0:D], xc[:], 0.0, None, ALU.max))
            dve.wait_ge(s_idx, 64)
            link(V.tensor_copy(idx_f[:], idx_i[:]))
            for n, (dst_t, src_p) in enumerate(((w1aT, pA[0:2 * D, 0:HID]), (weT, pB[0:D, 0:HID]), (w1bT, pC[0:HID, 0:D]),
                                                (w2aT, pD[0:2 * D, 0:HID]), (w2bT, pA[0:HID, 0:D]), (wrzT, pB[0:D, 0:D]),
                                                (wrhT, pC[0:D, 0:D]))):
                dve.wait_ge(s_tr, n + 1)
                V.tensor_copy(dst_t[:], src_p).then_inc(s_ev, 1)
            n = 7
            for k in range(K):
                for m, dst_t in enumerate((srcL, dstL)):
                    dve.wait_ge(s_tr, n + 1)
                    V.tensor_copy(dst_t[:, :, k], (pA, pB)[m][:, 0:NG]).then_inc(s_ev, 1)
                    n += 1
            for b in range(NB):
                dve.wait_ge(s_tr, n + 1)
                V.tensor_copy(hT[:, b, :], (pC, pD)[b % 2][0:D, 0:BN]).then_inc(s_ev, 1)
                n += 1
            dve.wait_ge(s_ev, n)
            MAGIC = 1.5 * 2 ** 23
            link(V.tensor_scalar(srcq[:], srcL[:], 1.0 / BN, 0.5 / BN - 0.5, ALU.mult, ALU.add))
            link(V.tensor_scalar(srcq[:], srcq[:], MAGIC, -MAGIC, ALU.add, ALU.add))
            link(V.scalar_tensor_tensor(mark[:], srcq[:], -float(BN), srcL[:], ALU.mult, ALU.add))
            link(V.tensor_scalar(mark[:], mark[:], 1.0, None, ALU.add))
            dve.wait_ge(s_iota, 2)
            link(V.reciprocal(rec_mark[:], rec_mark[:]))
            for b in range(NB):
                dve.wait_ge(s_proj, b + 1)
                if b >= 2:
                    dve.wait_ge(s_pst[b % 2], 16 * (b // 2))
                V.tensor_copy(proj[:, b % 2, :], (pA, pB)[b % 2][0:BN, 0:HID]).then_inc(s_pe_ev, 1)
            def group(g, first):
                if not first:
                    for k in range(K):
                        dve.wait_ge(s_g[k], g * 16)
                V.tensor_copy(dst_now[:], dstL[:, bass.ds(g, 1), :].rearrange("p a k -> p (a k)")).then_inc(s_stage, 1)
                for k in range(K):
                    dve.wait_ge(s_eT, g * K + k + 1)
                    V.tensor_copy(eaT[:], pA[0:D, 0:128]).then_inc(s_eTe, 1)
                    if k or not first:
                        dve.wait_ge(s_used, g * K + k)
                    V.tensor_scalar(onehot[:].rearrange("p b n -> p (b n)"), node_row[:],
                                    srcL[:, bass.ds(g, 1), k], None, ALU.is_equal)
                    V.tensor_copy(msg[:, D:MW], mark[:, bass.ds(g, 1), k])
                    dve.wait_ge(s_m, g * K + k + 1)
                    V.tensor_tensor(msg[:, 0:D], pC[:, 0:D], b1b_all[:], ALU.add).then_inc(s_me, 1)

            group(0, True)
            with dve.Fori(1, NG) as g:
                group(g, False)
            dve.wait_ge(s_used, NG * K)
            for b in range(NB):
                ins = V.tensor_copy(sums[:, b, :], acc_of(b))
            link(ins)
            link(V.tensor_scalar(cnt[:, 0, :], sums[:, :, D], rec_mark[0:BN, :], 1.0, ALU.mult, ALU.max))
            link(V.reciprocal(cnt[:, 1, :], cnt[:, 0, :]))
            V.tensor_tensor(h_agg[:, :, D:2 * D], sums[:, :, 0:D], cnt[:, 1, :].unsqueeze(2).to_broadcast(bc),
                            ALU.mult).then_inc(s_cat, 1)
            for b in range(NB):
                dve.wait_ge(s_ct, b + 1)
                V.tensor_copy(catT[:, b % 2, :], (pA, pB)[b % 2][0:2 * D, 0:BN]).then_inc(s_cte, 1)
                dve.wait_ge(s_z, b + 1)
                V.tensor_scalar(zT[:], pD[0:D, 0:BN], b2b_col[:], None, ALU.add).then_inc(s_ze, 1)
                dve.wait_ge(s_o, b + 1)
                link(V.tensor_tensor(ot[:, b, :], pC[0:BN, 0:D], xs[:, b, :], ALU.add))
                V.tensor_tensor(ot[:, b, :], ot[:, b, :], br_all[0:BN, :], ALU.add).then_inc(s_oe, 1)

        @block.scalar
        def _(act):
            A = nc.scalar
            act.wait_ge(s_v, 6)
            A.activation(stat[:, 2, :], stat[:, 1, :], ACT.Sqrt).then_inc(s_a, 1)
            with act.Fori(0, NG) as g:
                for k in range(K):
                    act.wait_ge(s_h, g * K + k + 1)
                    A.activation(rT[:], pB[:, 0:128], ACT.Relu).then_inc(s_r, 1)
            for b in range(NB):
                act.wait_ge(s_z1, b + 1)
                A.activation(z1T[:], pA[0:HID, 256:256 + BN], ACT.Relu, bias=b2a_col[:]).then_inc(s_z1e, 1)

        @block.tensor
        def _(pe):
            T = nc.tensor
            pe.wait_ge(s_w, 16 * NW)
            pe.wait_ge(s_id, 2)
            jobs = [(pA[0:2 * D, 0:HID], w1a_in[:]), (pB[0:D, 0:HID], w1a_in[:, D:2 * D]), (pC[0:HID, 0:D], w1b_in[:]),
                    (pD[0:2 * D, 0:HID], w2a_in[:]), (pA[0:HID, 0:D], w2b_in[:]), (pB[0:D, 0:D], wr_in[:, 0:D]),
                    (pC[0:D, 0:D], wr_in[:, D:2 * D])]
            for n, (o, a) in enumerate(jobs):
                if n >= 4:
                    pe.wait_ge(s_ev, n - 3)
                T.transpose(o, a, ident[0:a.shape[0], 0:a.shape[0]]).then_inc(s_tr, 1)
            n = 7
            pe.wait_ge(s_v, 10)
            pe.wait_ge(s_ev, 7)
            for k in range(K):
                for m in range(2):
                    if k:
                        pe.wait_ge(s_ev, n - 1)
                    T.transpose((pA, pB)[m][:, 0:NG], idx_f[:, m, :].rearrange("g (p k) -> g k p", k=K)[:, k, :],
                                ident[0:NG, 0:NG]).then_inc(s_tr, 1)
                    n += 1
            for b in range(NB):
                if b >= 2:
                    pe.wait_ge(s_ev, n - 1)
                T.transpose((pC, pD)[b % 2][0:D, 0:BN], h_agg[:, b, 0:D], ident[0:BN, 0:BN]).then_inc(s_tr, 1)
                n += 1
            pe.wait_ge(s_ev, n)
            pe.wait_ge(s_iota, 3)
            for b in range(NB):
                if b >= 2:
                    pe.wait_ge(s_pe_ev, b - 1)
                o = (pA, pB)[b % 2][0:BN, 0:HID]
                T.matmul(o, hT[:, b, :], w1aT[0:D, :], start=True, stop=False)
                T.matmul(o, ones_row[:, 0:BN], b1a_row[:], start=False, stop=True).then_inc(s_proj, 1)
            pe.wait_ge(s_pe_ev, NB)


            def group(g, slot, first):
                pe.wait_ge(s_ea[slot], ea_count(g, slot))
                pe.sem_inc(s_gate, 1)
                for k in range(K):
                    t = g * K + k
                    T.transpose(pA[0:D, 0:128], ea[:, slot, k, :], ident[:]).then_inc(s_eT, 1)
                    pe.wait_ge(s_g[k], g * 16 + 16)
                    T.matmul(pB[:, 0:128], pg[:, k, :], ident[:], start=True, stop=False)
                    pe.wait_ge(s_eTe, t + 1)
                    T.matmul(pB[:, 0:128], weT[:], eaT[:], start=False, stop=True).then_inc(s_h, 1)
                    pe.wait_ge(s_r, t + 1)
                    T.matmul(pC[:, 0:D], rT[:], w1bT[:], start=True, stop=True).then_inc(s_m, 1)
                    pe.wait_ge(s_me, t + 1)
                    for b in range(NB):
                        last = T.matmul(acc_of(b), onehot[:, b, :], msg[:], start=(first and k == 0 and b % PER_BANK == 0),
                                        stop=False, skip_group_check=True)
                    last.then_inc(s_used, 1)

            def ea_count(g, slot):
                return g * 8 + (16 if slot == 0 else 8)

            group(0, 0, True)
            group(1, 1, False)
            with pe.Fori(1, NG // 2 - 1) as i:
                group(i * 2, 0, False)
                group(i * 2 + 1, 1, False)
            group(NG - 2, 0, False)
            pe.wait_ge(s_ea[1], (NG // 2 + 1) * 16)
            group(NG - 1, 1, False)
            pe.wait_ge(s_cat, 1)
            for b in range(NB):
                if b >= 2:
                    pe.wait_ge(s_oe, b - 1)
                T.transpose((pA, pB)[b % 2][0:2 * D, 0:BN], h_agg[:, b, :], ident[0:BN, 0:BN]).then_inc(s_ct, 1)
                pe.wait_ge(s_cte, b + 1)
                T.matmul(pA[0:HID, 256:256 + BN], w2aT[:], catT[:, b % 2, :], start=True, stop=True).then_inc(s_z1, 1)
                pe.wait_ge(s_z1e, b + 1)
                T.matmul(pD[0:D, 0:BN], w2bT[:], z1T[:], start=True, stop=True).then_inc(s_z, 1)
                pe.wait_ge(s_ze, b + 1)
                T.matmul(pC[0:BN, 0:D], zT[:], wrzT[:], start=True, stop=False)
                T.matmul(pC[0:BN, 0:D], hT[:, b, :], wrhT[:], start=False, stop=True).then_inc(s_o, 1)


_INS = ['x', 'src', 'dst', 'edge_attr_64'] + ['L0_gnn_' + w for w in ('W1a', 'b1a', 'W1b', 'b1b', 'W2a', 'b2a', 'W2b', 'b2b', 'Wr', 'br')]


def kernel(**inputs):
    import numpy as np
    import concourse.bacc as bacc
    from concourse.bass_utils import run_bass_kernel_spmd
    nc = bacc.Bacc("TRN2", target_bir_lowering=False, num_devices=1)
    arrays, args = {}, []
    for name in _INS:
        a = np.ascontiguousarray(inputs[name])
        arrays[f"in_{name}"] = a
        args.append(nc.dram_tensor(f"in_{name}", a.shape, mybir.dt.from_np(a.dtype), kind="ExternalInput").ap())
    args.append(nc.dram_tensor("out_0", inputs['x'].shape, mybir.dt.float32, kind="ExternalOutput").ap())
    gnn_layer(nc, *args)
    r = run_bass_kernel_spmd(nc, [arrays], core_ids=[0])
    return r.results[0]["out_0"]
```

```python
import math
from contextlib import ExitStack

import concourse.bass as bass
from concourse import mybir



def gnn_layer(nc, x, src, dst, edge_attr, W1a, b1a, W1b, b1b, W2a, b2a, W2b, b2b, Wr, br, out):
    f32, i32, bf16 = mybir.dt.float32, mybir.dt.int32, mybir.dt.bfloat16
    ALU, ACT, AX = mybir.AluOpType, mybir.ActivationFunctionType, mybir.AxisListType

    N, D = x.shape
    E = src.shape[0]
    HID = W1a.shape[0]
    NB = 25
    BN = N // NB
    K = 8
    GE = 128 * K
    NG = (E + GE - 1) // GE
    NP = NG // 2
    PK = 2 * K
    LAST = E - (NG - 1) * GE
    LP, LR = LAST // K, LAST % K
    WS = 64
    NWIN = (N - 1) // WS + 1
    HC = (NWIN - 1) * WS + 128
    EPS = 1e-5
    MAGIC = 1.5 * 2 ** 23
    BIG = float(2 ** 18)

    P1 = 18
    BPP = 3

    def capacity(edges):
        mean = edges / NB
        return math.ceil((mean + BN + 4 * math.sqrt(mean)) / 128)

    C1 = capacity(P1 * 2 * GE - N * P1 // NP)
    C2 = capacity(E - P1 * 2 * GE - N * (NP - P1) // NP)
    FILL2 = -(-NB * C2 // (P1 - 1))
    SLOTS1 = NB * C1 * 128
    SLOTS = SLOTS1 + FILL2 * (P1 - 1) * 128
    RW = 3 * D + 2
    AW = 3 * D + 1
    NQ = NB + 1

    with ExitStack() as ctx:
        def sb(name, shape, dt=f32):
            return ctx.enter_context(nc.sbuf_tensor(name, shape, dt))

        def sem(name):
            return ctx.enter_context(nc.semaphore(name))

        ident = sb("ident", [128, 128])
        ident_b = sb("ident_b", [128, 128], bf16)
        below = sb("below", [128, 128], bf16)
        not_below = sb("not_below", [128, 128], bf16)
        ones_row = sb("ones_row", [1, 128])
        place = sb("place", [128, 1])
        rec_mark = sb("rec_mark", [128, 1])
        mark_row = sb("mark_row", [128, BN], bf16)
        bucket_row = sb("bucket_row", [128, NQ])
        restart = sb("restart", [128, NQ, PK])
        base = sb("base", [1, 2, NQ])
        w1a_in = sb("w1a_in", [HID, 2 * D])
        w1b_in = sb("w1b_in", [D, HID])
        w2a_in = sb("w2a_in", [HID, 2 * D])
        w2b_in = sb("w2b_in", [D, HID])
        wr_in = sb("wr_in", [D, 2 * D])
        w1aT = sb("w1aT", [2 * D, HID])
        we2T = sb("we2T", [2 * D, HID])
        w1bT = sb("w1bT", [HID, D])
        w2aT = sb("w2aT", [2 * D, HID])
        w2bT = sb("w2bT", [HID, D])
        wrzT = sb("wrzT", [D, D])
        wrhT = sb("wrhT", [D, D])
        b1b_all = sb("b1b_all", [128, D])
        br_all = sb("br_all", [128, D])
        b1a_col = sb("b1a_col", [HID, 1])
        b2a_col = sb("b2a_col", [HID, 1])
        b2b_col = sb("b2b_col", [D, 1])
        zeros = sb("zeros", [128, max(C1, FILL2) * RW], bf16)

        xs = sb("xs", [BN, NB, D])
        h = sb("h", [BN, NB, D])
        cat = sb("cat", [BN, 4, 2 * D])
        xc = sb("xc", [BN, NB, D])
        ot = sb("ot", [BN, NB, D])
        stat = sb("stat", [BN, 4, NB])
        hT = sb("hT", [D, HC])
        pwin = sb("pwin", [128, NWIN, 3, HID], bf16)
        rest = sb("rest", [128, 2, 512])
        sums = sb("sums", [BN, NB, D + 1])
        part2 = sb("part2", [BN, 4, D])
        cnt = sb("cnt", [BN, 4, 4])
        biased = sb("biased", [BN, 4, D])
        catT = sb("catT", [2 * D, 4 * BN])
        z1T = sb("z1T", [HID, 4 * BN])
        zT = sb("zT", [D, 4 * BN])

        idx_i = sb("idx_i", [NG, 2, GE], i32)
        idx_f = sb("idx_f", [NG, 2, GE])
        rel = sb("rel", [128, 2, 4, 128], bf16)
        wstat = sb("wstat", [NG, 4])
        win = sb("win", [1, NG], i32)
        bad = sb("bad", [1, 4])
        region_fill = sb("region_fill", [1, NQ])
        flag = sb("flag", [1, 1], i32)
        srcL = sb("srcL", [128, NG, K])
        srcq = sb("srcq", [128, NG, K])
        mark = sb("mark", [128, NG, K])
        limit = sb("limit", [128, NG, K])
        eq = sb("eq", [128, NQ, PK])
        incl = sb("incl", [128, NQ, PK])
        slot_t = sb("slot_t", [128, NQ, PK])
        rowcnt = sb("rowcnt", [128, NQ], bf16)
        pos = sb("pos", [128, 3, PK])
        pos_i = sb("pos_i", [128, 2, K], i32)
        ea = sb("ea", [128, 2, K, D])
        eaT = sb("eaT", [2 * D, 2, 512])
        oh = sb("oh", [128, 2, 2, 512], bf16)
        rT = sb("rT", [HID, 2, 512])
        r1 = sb("r1", [128, 2, K, D])
        pay = sb("pay", [128, 2, K, RW], bf16)
        rows = sb("rows", [128, 4, C1, RW], bf16)
        oh2 = sb("oh2", [128, 4, C1, BN], bf16)
        slots_dram = nc.dram_tensor("slots_dram", (SLOTS, RW), bf16, kind="Internal").ap()
        proj_dram = nc.dram_tensor("proj_dram", (N, HID), f32, kind="Internal").ap()

        old = pwin[:].rearrange("p w c h -> p (w c h)").bitcast(f32)
        node_row = old[:, 0:NB * BN]
        s_onehot = old[:, NB * BN:2 * NB * BN].rearrange("p (b n) -> p b n", n=BN)
        o = 2 * NB * BN
        pg = old[:, o:o + K * HID].rearrange("p (k h) -> p k h", h=HID)
        o += K * HID
        s_proj = old[0:BN, o:o + 2 * HID].rearrange("p (a h) -> p a h", h=HID)
        o += 2 * HID
        s_msg = old[:, o:o + D + 1]
        o += D + 2
        s_eaT = old[0:D, o:o + 128]
        o += 128
        s_rT = old[:, o:o + 128]
        s_src = srcL
        dstL = rows[:].rearrange("p a c w -> p (a c w)").bitcast(i32)[:, 0:NG * K].rearrange("p (g k) -> p g k", k=K)
        dst_now = rows[:].rearrange("p a c w -> p (a c w)").bitcast(i32)[:, NG * K:NG * K + K]

        bank = ctx.enter_context(nc.psum_tensor("bank", [128, 8, 512], f32))
        pT, pM, pR = bank[:, 0, :], bank[:, 1, :], bank[:, 2:4, :]
        pH = bank[:, 4:6, :]
        RANK = bank[:, 7, 0:NQ]

        def acc1(v):
            return bank[0:BN, 6, (v % 2) * AW:(v % 2) * AW + AW]

        def acc2(v):
            return bank[0:BN, 6 - v // 2, (v % 2) * AW:(v % 2) * AW + AW]

        def bucket_rows(a):
            return a.unsqueeze(2).to_broadcast((128, NQ, PK))

        PER_BANK = 7

        def slow_acc(b):
            c = (b % PER_BANK) * (D + 1)
            return bank[0:BN, 4 + b // PER_BANK, c:c + D + 1]

        names = dict(
            w_in="weights_loaded", x_in="x_loaded", idx_in="indices_loaded", pad="pads_set", id="identity_made",
            const="constants_made", zero="zeros_made", fill1="regions_1_cleared", fill2="regions_2_cleared", v="vector_step",
            sq="squares", sd="deviation", h="h_made", floats="indices_as_floats", setT="setup_transposed", setE="setup_evacuated",
            hTt="h_transposed", hTe="hT_evacuated", proj="windows_made", phi="windows_high", pr1="windows_rest",
            pmid="windows_middle", plo="windows_low", wready="windows_chosen", s_pre="src_prepared",
            T="edges_transposed", Te="edges_T_evacuated", Rb="rel_spread", oh="onehot_made", H="hidden_made", rl="hidden_relu",
            M="messages_made", hi="messages_high", r1="messages_rest", mid="messages_middle", payd="rows_ready", rc="row_counts",
            rk="ranks_made", rkr="ranks_read", rkd="ranks_moved_on", rkf="ranks_checked", oh2="sum_onehot_made", ag="block_summed",
            ae="block_sum_read", cat="mean_made", hc="h_beside_it", catT="cat_transposed", catE="cat_evacuated", z1="z1_made", z1e="z1_relu", z="z_made",
            ze="z_biased", o="out_made", oe="out_added", out="out_stored", flag="flag_set", gate="passed", pair="rank_step", batch="batch_step",
            again="mean_step")
        S = {k: sem(v) for k, v in names.items()}
        s_ea = [sem("edges_loaded_0"), sem("edges_loaded_1")]
        s_sc = [sem("rows_scattered_0"), sem("rows_scattered_1")]
        s_row = [sem(f"region_loaded_{v}") for v in range(4)]
        s_names = ("pj", "pje", "eT", "eTe", "H", "r", "M", "Me", "used", "stage", "iota", "dT", "dTe")
        L = {k: sem("slow_" + k) for k in s_names}
        l_pst = [sem("slow_projection_stored_0"), sem("slow_projection_stored_1")]
        l_g = [sem(f"slow_rows_gathered_{k}") for k in range(K)]
        l_ea = [sem("slow_edges_loaded_0"), sem("slow_edges_loaded_1")]
        n_sem = {k: sem("again_" + k) for k in ("cat", "hc", "catT", "catE", "z1", "z1e", "z", "ze", "o", "oe")}
        NODE = {k: S[k] for k in n_sem}
        NWT = 10
        PAIR_STEPS = 7
        MEAN_STEPS = 6
        BATCH_STEPS = 4 + MEAN_STEPS

        def edges_of(g):
            return edge_attr[bass.ds(g * GE, GE), :].rearrange("(p k) f -> p k f", k=K)

        def last_edges(sp, done):
            g0 = (NG - 1) * GE
            sp.dma_start(ea[0:LP, 1, :, :], edge_attr[g0:g0 + LP * K, :].rearrange("(p k) f -> p k f", k=K)).then_inc(done, 16)
            sp.dma_start(ea[LP:LP + 1, 1, 0:LR, :], edge_attr[g0 + LP * K:E, :].rearrange("(p k) f -> p k f", k=LR)).then_inc(done, 16)

        def region(ph, b, c):
            first = b * (c * 128) + (SLOTS1 if ph else 0)
            return slots_dram[bass.ds(first, c * 128), :].rearrange("(p t) w -> p t w", t=c)

        batches = [(4 * j, min(4, NB - 4 * j)) for j in range((NB + 3) // 4)]
        NJ = len(batches)

        block = ctx.enter_context(nc.Block())

        @block.sync
        def _(sp):
            sp.dma_start(xs[:], x.rearrange("(b p) f -> p b f", p=BN)).then_inc(S["x_in"], 16)
            sp.wait_ge(S["pad"], 1)
            for n, a in enumerate((src, dst)):
                sp.dma_start(idx_i[0:NG - 1, n, :], a[0:(NG - 1) * GE].rearrange("(g e) -> g e", e=GE)).then_inc(S["idx_in"], 16)
                sp.dma_start(idx_i[NG - 1:NG, n, 0:LAST], a[(NG - 1) * GE:E].rearrange("(g e) -> g e", g=1)).then_inc(S["idx_in"], 16)
            for t, a in ((w1a_in, W1a), (w1b_in, W1b), (w2a_in, W2a), (w2b_in, W2b), (wr_in, Wr)):
                sp.dma_start(t[:], a).then_inc(S["w_in"], 16)
            for t, a in ((b1b_all, b1b), (br_all, br)):
                sp.dma_start(t[:], a.rearrange("(o n) -> o n", o=1).to_broadcast((128, D))).then_inc(S["w_in"], 16)
            for t, a in ((b1a_col, b1a), (b2a_col, b2a), (b2b_col, b2b)):
                sp.dma_start(t[:], a.rearrange("(n o) -> n o", o=1)).then_inc(S["w_in"], 16)
            for g in range(2):
                sp.dma_start(ea[:, g, :, :], edges_of(g)).then_inc(s_ea[g], 16)
            sp.wait_ge(S["zero"], 1)
            for b in range(NB):
                sp.dma_start(region(0, b, C1).rearrange("p t w -> p (t w)"), zeros[:, 0:C1 * RW]).then_inc(S["fill1"], 16)

            def load(g, u):
                sp.wait_ge(S["T"], g - 1)
                sp.dma_start(ea[:, u, :, :], edges_of(g)).then_inc(s_ea[u], 16)

            load(2, 0)
            load(3, 1)
            with sp.Fori(1, P1) as i:
                load(i * 2 + 2, 0)
                first = (i - 1) * (FILL2 * 128) + SLOTS1
                sp.dma_start(slots_dram[bass.ds(first, FILL2 * 128), :].rearrange("(p t) w -> p (t w)", p=128),
                             zeros[:, 0:FILL2 * RW]).then_inc(S["fill2"], 16)
                load(i * 2 + 3, 1)
            for u in range(2):
                sp.wait_ge(s_sc[u], 16 * K * P1)

            def load_blocks(i, first):
                for v in range(BPP):
                    if not first:
                        sp.wait_ge(S["ag"], (i - P1) * BPP - BPP + v + 1)
                    sp.dma_start(rows[:, v, :, :], region(0, (i - P1) * BPP + v, C1)).then_inc(s_row[v], 16)

            load_blocks(P1, True)
            load(P1 * 2 + 2, 0)
            load(P1 * 2 + 3, 1)
            with sp.Fori(P1 + 1, NP - 2) as i:
                load(i * 2 + 2, 0)
                load_blocks(i, False)
                load(i * 2 + 3, 1)
            load(NG - 2, 0)
            load_blocks(NP - 2, False)
            sp.wait_ge(S["T"], NG - 2)
            last_edges(sp, s_ea[1])
            load_blocks(NP - 1, False)
            done = BPP * (NP - P1)
            for v in range(NB - done):
                sp.wait_ge(S["ag"], done - BPP + v + 1)
                sp.dma_start(rows[:, v, :, :], region(0, done + v, C1)).then_inc(s_row[v], 16)
            for u in range(2):
                sp.wait_ge(s_sc[u], 16 * K * NP)

            def load_batch(b0, n):
                for v in range(n):
                    sp.wait_ge(S["ag"], NB + b0 - 4 + v + 1 if not isinstance(b0, int) or b0 else NB)
                    sp.dma_start(rows[:, v, 0:C2, :], region(1, b0 + v, C2)).then_inc(s_row[v], 16)

            load_batch(0, 4)
            with sp.Fori(1, NJ - 1) as j:
                load_batch(j * 4, 4)
            load_batch(*batches[-1])
            sp.wait_ge(S["oe"], NJ)
            sp.dma_start(out.rearrange("(b p) f -> p b f", p=BN), ot[:]).then_inc(S["out"], 16)
            sp.wait_ge(S["out"], 16)
            sp.wait_ge(S["flag"], 1)
            is_bad = sp.value_load(flag[0:1, 0:1], min_val=0, max_val=1)
            with sp.If(is_bad > 0):
                for b in range(NB):
                    sp.wait_ge(L["pje"], b + 1)
                    sp.dma_start(proj_dram[b * BN:(b + 1) * BN, :], s_proj[:, b % 2, :]).then_inc(l_pst[b % 2], 16)
                for g in range(2):
                    sp.dma_start(ea[:, g, :, :], edges_of(g)).then_inc(l_ea[g], 16)

                def slow_load(g, u):
                    sp.wait_ge(L["used"], g * K - K)
                    sp.dma_start(ea[:, u, :, :], edges_of(g)).then_inc(l_ea[u], 16)

                with sp.Fori(1, NP - 1) as i:
                    slow_load(i * 2, 0)
                    slow_load(i * 2 + 1, 1)
                slow_load(NG - 2, 0)
                sp.wait_ge(L["used"], (NG - 2) * K)
                last_edges(sp, l_ea[1])
                sp.wait_ge(n_sem["oe"], NJ)
                sp.dma_start(out.rearrange("(b p) f -> p b f", p=BN), ot[:]).then_inc(S["out"], 16)
                sp.wait_ge(S["out"], 32)
            sp.sem_inc(S["gate"], 1)

        @block.gpsimd
        def _(pool):
            G = nc.gpsimd
            G.memset(idx_i[:, 0, :], NB * BN)
            G.memset(idx_i[:, 1, :], N - 1).then_inc(S["pad"], 1)
            G.memset(zeros[:], 0.0).then_inc(S["zero"], 1)
            G.memset(ident[:], 0.0)
            G.memset(below[:], 1.0)
            G.memset(not_below[:], 1.0)
            G.memset(restart[:], 1.0).then_inc(S["id"], 1)
            pool.wait_ge(S["id"], 1)
            G.affine_select(out=ident[:], in_=ident[:], compare_op=ALU.not_equal, fill=1.0, base=0,
                            pattern=[[-1, 128]], channel_multiplier=1)
            G.affine_select(out=below[:], in_=below[:], compare_op=ALU.is_gt, fill=0.0, base=0,
                            pattern=[[1, 128]], channel_multiplier=-1)
            G.affine_select(out=not_below[:], in_=not_below[:], compare_op=ALU.is_ge, fill=0.0, base=0,
                            pattern=[[-1, 128]], channel_multiplier=1)
            G.memset(restart[:, :, 0:1], 0.0).then_inc(S["id"], 1)

            def count(t, pattern, first, down):
                return G.iota(t, pattern=pattern, base=first, channel_multiplier=down, allow_small_or_imprecise_dtypes=True)

            count(place[:], [[0, 1]], 0, 1)
            count(rec_mark[:], [[0, 1]], 1, 1)
            count(mark_row[:], [[1, BN]], 1, 0)
            count(bucket_row[:], [[1, NQ]], 0, 0)
            count(base[:, 0, :], [[C1 * 128, NQ]], -1, 0)
            count(base[:, 1, :], [[C2 * 128, NQ]], SLOTS1 - 1, 0)
            G.memset(pay[:], 0.0)
            G.memset(rel[:], 0.0)
            G.memset(hT[:], 0.0)
            G.memset(ones_row[:], 1.0).then_inc(S["const"], 1)
            pool.wait_ge(S["id"], 2)
            G.tensor_copy(ident_b[:], ident[:]).then_inc(S["const"], 1)

            def scatter(i, u):
                pool.wait_ge(S["payd"], i * 2 + u + 1)
                pool.sem_inc(S["gate"], 1)
                for k in range(K):
                    pool.indirect_dma_start(out=slots_dram[:, :], out_offset=bass.IndirectOffsetOnAxis(ap=pos_i[:, u, k:k + 1], axis=0),
                                            in_=pay[:, u, k, :], in_offset=None, bounds_check=SLOTS - 1, oob_is_err=False
                                            ).then_inc(s_sc[u], 16)

            pool.wait_ge(S["fill1"], 16 * NB)
            with pool.Fori(0, P1) as i:
                scatter(i, 0)
                scatter(i, 1)
            pool.wait_ge(S["fill2"], 16 * (P1 - 1))
            with pool.Fori(P1, NP) as i:
                scatter(i, 0)
                scatter(i, 1)

            pool.wait_ge(S["flag"], 1)
            is_bad = pool.value_load(flag[0:1, 0:1], min_val=0, max_val=1)
            with pool.If(is_bad > 0):
                G.iota(node_row, pattern=[[1, NB * BN]], base=0, channel_multiplier=0,
                       allow_small_or_imprecise_dtypes=True).then_inc(L["iota"], 1)
                pool.wait_ge(l_pst[0], 16 * ((NB + 1) // 2))
                pool.wait_ge(l_pst[1], 16 * (NB // 2))
                with pool.Fori(0, NG) as g:
                    pool.wait_ge(L["stage"], g + 1)
                    pool.sem_inc(S["gate"], 1)
                    for k in range(K):
                        pool.indirect_dma_start(out=pg[:, k, :], out_offset=None, in_=proj_dram,
                                                in_offset=bass.IndirectOffsetOnAxis(ap=dst_now[:, k:k + 1], axis=0)
                                                ).then_inc(l_g[k], 16)
            pool.sem_inc(S["gate"], 1)

        @block.vector
        def _(dve):
            V = nc.vector
            done = [0]

            def link(ins):
                done[0] += 1
                ins.then_inc(S["v"], 1)
                dve.wait_ge(S["v"], done[0])

            bc = (BN, NB, D)
            dve.wait_ge(S["idx_in"], 64)
            V.tensor_copy(idx_f[:], idx_i[:]).then_inc(S["floats"], 1)
            dve.wait_ge(S["x_in"], 16)
            link(V.tensor_reduce(stat[:, 0, :], xs[:], axis=AX.X, op=ALU.add))
            link(V.tensor_scalar(stat[:, 0, :], stat[:, 0, :], 1.0 / D, None, ALU.mult))
            link(V.tensor_tensor(xc[:], xs[:], stat[:, 0, :].unsqueeze(2).to_broadcast(bc), ALU.subtract))
            dve.wait_ge(S["sq"], 1)
            link(V.tensor_reduce(stat[:, 1, :], ot[:], axis=AX.X, op=ALU.add))
            link(V.tensor_scalar(stat[:, 1, :], stat[:, 1, :], 1.0 / D, EPS, ALU.mult, ALU.add))
            dve.wait_ge(S["floats"], 1)
            dstF = idx_f[:, 1, :]
            V.tensor_reduce(wstat[:, 0:1], dstF, axis=AX.X, op=ALU.min)
            link(V.tensor_reduce(wstat[:, 1:2], dstF, axis=AX.X, op=ALU.max))
            link(V.tensor_scalar(wstat[:, 2:3], wstat[:, 0:1], 1.0 / WS, 0.5 / WS - 0.5, ALU.mult, ALU.add))
            link(V.tensor_scalar(wstat[:, 2:3], wstat[:, 2:3], MAGIC, -MAGIC, ALU.add, ALU.add))
            link(V.tensor_scalar(wstat[:, 0:1], wstat[:, 2:3], float(WS), None, ALU.mult))
            link(V.tensor_tensor(wstat[:, 3:4], wstat[:, 1:2], wstat[:, 0:1], ALU.subtract))
            dve.wait_ge(S["const"], 1)
            V.tensor_scalar(rel[0:NG].rearrange("g r j p -> g p j r"), dstF.rearrange("g (p j r) -> g p j r", j=4, r=2),
                            wstat[:, 0:1], None, ALU.subtract).then_inc(S["wready"], 1)
            dve.wait_ge(S["sd"], 1)
            link(V.reciprocal(stat[:, 3, :], stat[:, 2, :]))
            link(V.tensor_tensor(xc[:], xc[:], stat[:, 3, :].unsqueeze(2).to_broadcast(bc), ALU.mult))
            V.tensor_scalar(h[:], xc[:], 0.0, None, ALU.max).then_inc(S["h"], 1)
            link(V.reciprocal(rec_mark[:], rec_mark[:]))
            V.memset(base[:, :, NB:NQ], BIG)

            dve.wait_ge(S["setT"], 1)
            V.tensor_copy(w1aT[:], bank[:, 0, 0:HID])
            V.tensor_copy(we2T[0:D, :], bank[0:D, 0, 128:128 + HID])
            V.tensor_copy(we2T[D:2 * D, :], bank[D:2 * D, 0, 0:HID])
            V.tensor_copy(w1bT[:], bank[:, 0, 256:256 + D])
            V.tensor_copy(w2aT[:], bank[:, 0, 384:384 + HID])
            V.tensor_copy(w2bT[:], bank[:, 1, 0:D])
            V.tensor_copy(wrzT[:], bank[0:D, 1, 128:128 + D])
            V.tensor_copy(wrhT[:], bank[0:D, 1, 256:256 + D]).then_inc(S["setE"], 1)
            dve.wait_ge(S["setT"], 2)
            link(V.tensor_copy(srcL[:].rearrange("p g k -> p k g"), bank[:, 2, 0:K * NG].rearrange("p (k g) -> p k g", g=NG)))
            V.tensor_copy(win[:], bank[0:1, 3, 0:NG])
            link(V.tensor_reduce(bad[:, 0:1], bank[0:1, 3, 128:128 + NG], axis=AX.X, op=ALU.max))
            link(V.tensor_scalar(bad[:, 0:1], bad[:, 0:1], 127.5, None, ALU.is_gt))
            link(V.tensor_scalar(srcq[:], srcL[:], 1.0 / BN, 0.5 / BN - 0.5, ALU.mult, ALU.add))
            link(V.tensor_scalar(srcq[:], srcq[:], MAGIC, -MAGIC, ALU.add, ALU.add))
            V.tensor_scalar(limit[:, 0:2 * P1, :], srcq[:, 0:2 * P1, :], float(C1 * 128), C1 * 128 - 1.0, ALU.mult, ALU.add)
            V.tensor_scalar(limit[:, 2 * P1:NG, :], srcq[:, 2 * P1:NG, :], float(C2 * 128), SLOTS1 + C2 * 128 - 1.0, ALU.mult, ALU.add)
            link(V.scalar_tensor_tensor(mark[:], srcq[:], -float(BN), srcL[:], ALU.mult, ALU.add))
            V.tensor_scalar(mark[:], mark[:], 1.0, None, ALU.add).then_inc(S["setE"], 1)
            for j, (b0, n) in enumerate(batches):
                dve.wait_ge(S["hTt"], j + 1)
                V.tensor_copy(hT[:, b0 * BN:(b0 + n) * BN], bank[0:D, 4 + j % 4, 0:n * BN]).then_inc(S["hTe"], 1)
            dve.wait_ge(S["w_in"], 16 * NWT)
            V.tensor_tensor(xs[:], xs[:], br_all[0:BN, :].unsqueeze(1).to_broadcast(bc), ALU.add)
            for j in range((NWIN + 3) // 4):
                w0, n = 4 * j, min(4, NWIN - 4 * j)
                rj = rest[:, j % 2, 0:n * 128]
                view = rj.rearrange("p (w h) -> p w h", h=HID)
                dve.wait_ge(S["phi"], j + 1)
                V.tensor_tensor(view, bank[:, 4 + j % 4, 0:n * 128].rearrange("p (w h) -> p w h", h=HID),
                                pwin[:, w0:w0 + n, 0, :], ALU.subtract).then_inc(S["pr1"], 1)
                dve.wait_ge(S["pmid"], j + 1)
                V.tensor_tensor(pwin[:, w0:w0 + n, 2, :], view, pwin[:, w0:w0 + n, 1, :], ALU.subtract).then_inc(S["plo"], 1)

            def chain(i, of, per):
                n = [0]

                def step(ins):
                    n[0] += 1
                    ins.then_inc(of, 1)
                    dve.wait_ge(of, i * per + n[0])

                return step

            def onehot(g, u):
                dve.wait_ge(S["Rb"], g + 1)
                if not isinstance(g, int) or g >= 2:
                    dve.wait_ge(S["H"], (g - 1) * 2)
                V.tensor_scalar(oh[:, u, :, :], pR, place[:], None, ALU.is_equal).then_inc(S["oh"], 1)

            def ranks_a(i, step):
                if not isinstance(i, int) or i:
                    dve.wait_ge(S["payd"], i * 2)
                q = srcq[:, bass.ds(i * 2, 2), :].rearrange("p g k -> p (g k)")
                step(V.tensor_tensor(eq[:], q.unsqueeze(1).to_broadcast((128, NQ, PK)), bucket_rows(bucket_row[:]), ALU.is_equal))
                flat = "p b k -> p (b k)"
                step(V.tensor_tensor_scan(incl[:].rearrange(flat), restart[:].rearrange(flat), eq[:].rearrange(flat), 0.0,
                                          ALU.mult, ALU.add))
                if not isinstance(i, int) or i:
                    dve.wait_ge(S["rkd"], i)
                V.tensor_copy(rowcnt[:], incl[:, :, PK - 1]).then_inc(S["rc"], 1)

            def ranks_b(i, step):
                dve.wait_ge(S["rk"], i + 1)
                step(V.tensor_tensor(slot_t[:], incl[:], bucket_rows(RANK), ALU.add))
                step(V.tensor_tensor(slot_t[:], slot_t[:], eq[:], ALU.mult))
                step(V.tensor_reduce(pos[:, 0, :], slot_t[:].rearrange("p b k -> p k b"), axis=AX.X, op=ALU.add))
                lim = limit[:, bass.ds(i * 2, 2), :].rearrange("p g k -> p (g k)")
                step(V.tensor_tensor(pos[:, 1, :], pos[:, 0, :], lim, ALU.is_gt))
                step(V.scalar_tensor_tensor(pos[:, 2, :], pos[:, 1, :], BIG, pos[:, 0, :], ALU.mult, ALU.add))

            def payload(g, u):
                dve.wait_ge(S["hi"], g + 1)
                m = pM.rearrange("p (k f) -> p k f", f=D)
                V.tensor_tensor(r1[:, u, :, :], m, pay[:, u, :, 0:D], ALU.subtract).then_inc(S["r1"], 1)
                V.tensor_copy(pos_i[:, u, :], pos[:, 2, u * K:(u + 1) * K])
                V.tensor_copy(pay[:, u, :, 3 * D], mark[:, bass.ds(g, 1), :].rearrange("p g k -> p (g k)"))
                dve.wait_ge(S["mid"], g + 1)
                V.tensor_tensor(pay[:, u, :, 2 * D:3 * D], r1[:, u, :, :], pay[:, u, :, D:2 * D], ALU.subtract).then_inc(S["payd"], 1)

            def sum_onehot(v, use, c):
                dve.wait_ge(s_row[v], use * 16)
                V.tensor_tensor(oh2[:, v, 0:c, :], mark_row[:].unsqueeze(1).to_broadcast((128, c, BN)),
                                rows[:, v, 0:c, 3 * D:3 * D + 1].to_broadcast((128, c, BN)), ALU.is_equal).then_inc(S["oh2"], 1)

            def take_sums1(n, m):
                dve.wait_ge(S["ag"], n + m)
                a = bank[0:BN, 6, 0:m * AW].rearrange("p (v w) -> p v w", w=AW)
                V.tensor_reduce(sums[:, bass.ds(n, m), 0:D], a[:, :, 0:3 * D].rearrange("p v (c f) -> p v f c", c=3), axis=AX.X, op=ALU.add)
                V.tensor_copy(sums[:, bass.ds(n, m), D], a[:, :, 3 * D]).then_inc(S["ae"], 1)

            def pair(i, last=False, blocks=None):
                step = chain(i, S["pair"], PAIR_STEPS)
                ranks_a(i, step)
                onehot(i * 2 + 1, 1)
                if blocks:
                    sum_onehot(0, i - (P1 - 1), C1)
                    sum_onehot(1, i - (P1 - 1), C1)
                ranks_b(i, step)
                payload(i * 2, 0)
                if blocks:
                    take_sums1((i - P1) * BPP, 2)
                    sum_onehot(2, i - (P1 - 1), C1)
                if not last:
                    onehot(i * 2 + 2, 0)
                payload(i * 2 + 1, 1)
                if blocks:
                    take_sums1((i - P1) * BPP + 2, 1)

            def check_ranks(ph, c):
                link(V.tensor_tensor(region_fill[:], RANK[0:1, :], base[:, ph, :], ALU.subtract))
                link(V.tensor_reduce(bad[:, 1 + ph:2 + ph], region_fill[:, 0:NB], axis=AX.X, op=ALU.max))
                link(V.tensor_scalar(bad[:, 1 + ph:2 + ph], bad[:, 1 + ph:2 + ph], c * 128 + 0.5, None, ALU.is_gt))

            onehot(0, 0)
            pair(0)
            with dve.Fori(1, P1) as i:
                pair(i)
            dve.wait_ge(S["rkd"], P1)
            check_ranks(0, C1)
            V.memset(bad[:, 3:4], 0.0).then_inc(S["rkf"], 1)
            with dve.Fori(P1, NP - 1) as i:
                pair(i, blocks=True)
            pair(NP - 1, last=True, blocks=True)
            n1 = BPP * (NP - P1)
            for v in range(NB - n1):
                sum_onehot(v, NP - P1 + 1, C1)
                take_sums1(n1 + v, 1)
            dve.wait_ge(S["rkd"], NP)
            check_ranks(1, C2)

            uses = [NP - P1 + 1 if v < NB - n1 else NP - P1 if v < BPP else 0 for v in range(4)]
            assert NB - n1 <= BPP

            def batch_onehots(j, n):
                for v in range(n):
                    sum_onehot(v, j + (uses[v] + 1), C2)

            def take_sums2(j, n, step):
                b0 = j * 4
                for v0 in range(0, n, 2):
                    m = min(2, n - v0)
                    dve.wait_ge(S["ag"], b0 + NB + v0 + m)
                    a = bank[0:BN, 6 - v0 // 2, 0:m * AW].rearrange("p (v w) -> p v w", w=AW)
                    step(V.tensor_reduce(part2[:, v0:v0 + m, :], a[:, :, 0:3 * D].rearrange("p v (c f) -> p v f c", c=3), axis=AX.X, op=ALU.add))
                    d = sums[:, bass.ds(b0 + v0, m), :]
                    V.tensor_tensor(d[:, :, D], d[:, :, D], a[:, :, 3 * D], ALU.add)
                    step(V.tensor_tensor(d[:, :, 0:D], d[:, :, 0:D], part2[:, v0:v0 + m, :], ALU.add))

            def means(j, n, step, q):
                d = sums[:, bass.ds(j * 4, n), :]
                step(V.tensor_scalar(cnt[:, 0, 0:n], d[:, :, D], rec_mark[0:BN, :], MAGIC, ALU.mult, ALU.add))
                step(V.tensor_scalar(cnt[:, 1, 0:n], cnt[:, 0, 0:n], -MAGIC, None, ALU.add))
                step(V.tensor_scalar(cnt[:, 2, 0:n], cnt[:, 1, 0:n], 1.0, None, ALU.max))
                step(V.reciprocal(cnt[:, 3, 0:n], cnt[:, 2, 0:n]))
                s = (BN, n, D)
                step(V.tensor_tensor(biased[:, 0:n, :], b1b_all[0:BN, :].unsqueeze(1).to_broadcast(s),
                                     cnt[:, 1, 0:n].unsqueeze(2).to_broadcast(s), ALU.mult))
                step(V.tensor_tensor(biased[:, 0:n, :], biased[:, 0:n, :], d[:, :, 0:D], ALU.add))
                if not isinstance(j, int) or j:
                    dve.wait_ge(q["catT"], j)
                V.tensor_tensor(cat[:, 0:n, D:2 * D], biased[:, 0:n, :],
                                cnt[:, 3, 0:n].unsqueeze(2).to_broadcast(s), ALU.mult).then_inc(q["cat"], 1)

            def node(j, n, q):
                dve.wait_ge(q["catT"], j + 1)
                V.tensor_copy(catT[:, 0:n * BN], bank[:, 0, 0:n * BN]).then_inc(q["catE"], 1)
                dve.wait_ge(q["z"], j + 1)
                V.tensor_scalar(zT[:, 0:n * BN], bank[0:D, 2, 0:n * BN], b2b_col[:], None, ALU.add).then_inc(q["ze"], 1)
                dve.wait_ge(q["o"], j + 1)
                V.tensor_tensor(ot[:, bass.ds(j * 4, n), :], bank[0:BN, 3, 0:n * D].rearrange("p (v f) -> p v f", f=D),
                                xs[:, bass.ds(j * 4, n), :], ALU.add).then_inc(q["oe"], 1)

            def batch(j, n):
                step = chain(j, S["batch"], BATCH_STEPS)
                batch_onehots(j, n)
                take_sums2(j, n, step)
                means(j, n, step, NODE)

            batch(0, 4)
            with dve.Fori(1, NJ - 1) as j:
                batch(j, 4)
                node(j - 1, 4, NODE)
            batch(NJ - 1, batches[-1][1])
            node(NJ - 2, 4, NODE)
            node(NJ - 1, batches[-1][1], NODE)
            link(V.tensor_reduce(bad[:, 3:4], bad[:, 0:3], axis=AX.X, op=ALU.max))
            V.tensor_copy(flag[:], bad[:, 3:4]).then_inc(S["flag"], 1)
            dve.wait_ge(S["flag"], 1)
            is_bad = dve.value_load(flag[0:1, 0:1], min_val=0, max_val=1)
            with dve.If(is_bad > 0):
                dve.wait_ge(L["dT"], 1)
                V.tensor_copy(dstL.rearrange("p g k -> p k g"), bank[:, 0, 0:K * NG].rearrange("p (k g) -> p k g", g=NG)).then_inc(L["dTe"], 1)
                for b in range(NB):
                    dve.wait_ge(L["pj"], b + 1)
                    if b >= 2:
                        dve.wait_ge(l_pst[b % 2], 16 * (b // 2))
                    V.tensor_copy(s_proj[:, b % 2, :], bank[0:BN, b % 2, 0:HID]).then_inc(L["pje"], 1)
                dve.wait_ge(L["iota"], 1)
                dve.wait_ge(L["dTe"], 1)

                def group(g, first):
                    if not first:
                        for k in range(K):
                            dve.wait_ge(l_g[k], g * 16)
                    V.tensor_copy(dst_now, dstL[:, bass.ds(g, 1), :].rearrange("p a k -> p (a k)")).then_inc(L["stage"], 1)
                    for k in range(K):
                        dve.wait_ge(L["eT"], g * K + k + 1)
                        V.tensor_copy(s_eaT, bank[0:D, 0, 0:128]).then_inc(L["eTe"], 1)
                        if k or not first:
                            dve.wait_ge(L["used"], g * K + k)
                        V.tensor_scalar(s_onehot.rearrange("p b n -> p (b n)"), node_row,
                                        srcL[:, bass.ds(g, 1), k], None, ALU.is_equal)
                        V.tensor_copy(s_msg[:, D:D + 1], mark[:, bass.ds(g, 1), k])
                        dve.wait_ge(L["M"], g * K + k + 1)
                        V.tensor_copy(s_msg[:, 0:D], bank[:, 2, 0:D]).then_inc(L["Me"], 1)

                group(0, True)
                with dve.Fori(1, NG) as g:
                    group(g, False)
                dve.wait_ge(L["used"], NG * K)
                for b in range(NB):
                    last = V.tensor_copy(sums[:, b, :], slow_acc(b))
                last.then_inc(L["Me"], 1)
                dve.wait_ge(L["Me"], NG * K + 1)
                for j, (b0, n) in enumerate(batches):
                    means(j, n, chain(j, S["again"], MEAN_STEPS), n_sem)
                    node(j, n, n_sem)
            dve.sem_inc(S["gate"], 1)

        @block.scalar
        def _(act):
            A = nc.scalar
            act.wait_ge(S["v"], 3)
            A.activation(ot[:], xc[:], ACT.Square).then_inc(S["sq"], 1)
            act.wait_ge(S["v"], 5)
            A.activation(stat[:, 2, :], stat[:, 1, :], ACT.Sqrt).then_inc(S["sd"], 1)
            for j in range((NWIN + 3) // 4):
                w0, n = 4 * j, min(4, NWIN - 4 * j)
                act.wait_ge(S["proj"], j + 1)
                A.copy(pwin[:, w0:w0 + n, 0, :], bank[:, 4 + j % 4, 0:n * 128].rearrange("p (w h) -> p w h", h=HID)).then_inc(S["phi"], 1)
                act.wait_ge(S["pr1"], j + 1)
                A.copy(pwin[:, w0:w0 + n, 1, :], rest[:, j % 2, 0:n * 128].rearrange("p (w h) -> p w h", h=HID)).then_inc(S["pmid"], 1)

            def evacuate(g, u):
                act.wait_ge(S["T"], g + 1)
                if not isinstance(g, int) or g >= 2:
                    act.wait_ge(S["H"], (g - 1) * 2)
                A.copy(eaT[:, u, :], pT).then_inc(S["Te"], 1)

            def group(g, u, i, first, last):
                if not last:
                    evacuate(g + 1, 1 - u)
                for par in range(2):
                    act.wait_ge(S["H"], g * 2 + par + 1)
                    if not (first and u == 0):
                        act.wait_ge(S["M"], g * 2 + par - 1)
                    A.activation(rT[:, par, :], pH[:, par, :], ACT.Relu, bias=b1a_col[:]).then_inc(S["rl"], 1)
                act.wait_ge(S["M"], g * 2 + 2)
                if not first:
                    act.wait_ge(s_sc[u], i * (16 * K))
                A.copy(pay[:, u, :, 0:D], pM.rearrange("p (k f) -> p k f", f=D)).then_inc(S["hi"], 1)
                act.wait_ge(S["r1"], g + 1)
                A.copy(pay[:, u, :, D:2 * D], r1[:, u, :, :]).then_inc(S["mid"], 1)

            act.wait_ge(S["const"], 1)
            act.wait_ge(S["w_in"], 16 * NWT)
            evacuate(0, 0)
            group(0, 0, 0, True, False)
            group(1, 1, 0, True, False)
            with act.Fori(1, NP - 1) as i:
                group(i * 2, 0, i, False, False)
                group(i * 2 + 1, 1, i, False, False)
            group(NG - 2, 0, NP - 1, False, False)
            group(NG - 1, 1, NP - 1, False, True)

            def take_h(j, n, q):
                if not isinstance(j, int) or j:
                    act.wait_ge(q["catT"], j)
                A.copy(cat[:, 0:n, 0:D], h[:, bass.ds(j * 4, n), :]).then_inc(q["hc"], 1)

            def node(j, n, q):
                act.wait_ge(q["z1"], j + 1)
                A.activation(z1T[:, 0:n * BN], bank[:, 1, 0:n * BN], ACT.Relu, bias=b2a_col[:]).then_inc(q["z1e"], 1)

            take_h(0, 4, NODE)
            with act.Fori(1, NJ - 1) as j:
                take_h(j, 4, NODE)
                node(j - 1, 4, NODE)
            take_h(NJ - 1, batches[-1][1], NODE)
            node(NJ - 2, 4, NODE)
            node(NJ - 1, batches[-1][1], NODE)
            act.wait_ge(S["flag"], 1)
            is_bad = act.value_load(flag[0:1, 0:1], min_val=0, max_val=1)
            with act.If(is_bad > 0):
                with act.Fori(0, NG) as g:
                    for k in range(K):
                        act.wait_ge(L["H"], g * K + k + 1)
                        A.activation(s_rT, bank[:, 1, 0:128], ACT.Relu, bias=b1a_col[:]).then_inc(L["r"], 1)
                for j, (b0, n) in enumerate(batches):
                    take_h(j, n, n_sem)
                    node(j, n, n_sem)
            act.sem_inc(S["gate"], 1)

        @block.tensor
        def _(pe):
            T = nc.tensor
            pe.wait_ge(S["w_in"], 16 * NWT)
            pe.wait_ge(S["id"], 2)
            I = ident
            T.transpose(bank[:, 0, 0:HID], w1a_in[:], I[:])
            T.transpose(bank[0:D, 0, 128:128 + HID], w1a_in[:, D:2 * D], I[:])
            T.transpose(bank[:, 0, 256:256 + D], w1b_in[:], I[0:D, 0:D])
            T.transpose(bank[:, 0, 384:384 + HID], w2a_in[:], I[:])
            T.transpose(bank[:, 1, 0:D], w2b_in[:], I[0:D, 0:D])
            T.transpose(bank[0:D, 1, 128:128 + D], wr_in[:, 0:D], I[0:D, 0:D])
            T.transpose(bank[0:D, 1, 256:256 + D], wr_in[:, D:2 * D], I[0:D, 0:D]).then_inc(S["setT"], 1)
            pe.wait_ge(S["floats"], 1)
            for k in range(K):
                T.transpose(bank[:, 2, k * NG:(k + 1) * NG], idx_f[:, 0, :].rearrange("g (p k) -> g k p", k=K)[:, k, :], I[0:NG, 0:NG])
            pe.wait_ge(S["wready"], 1)
            T.transpose(bank[0:1, 3, 0:NG], wstat[:, 2:3], I[0:NG, 0:NG])
            T.transpose(bank[0:1, 3, 128:128 + NG], wstat[:, 3:4], I[0:NG, 0:NG]).then_inc(S["setT"], 1)
            pe.wait_ge(S["h"], 1)
            for j, (b0, n) in enumerate(batches):
                if j >= 4:
                    pe.wait_ge(S["hTe"], j - 3)
                for v in range(n):
                    last = T.transpose(bank[0:D, 4 + j % 4, v * BN:(v + 1) * BN], h[:, b0 + v, :], I[0:BN, 0:BN])
                last.then_inc(S["hTt"], 1)
            pe.wait_ge(S["hTe"], NJ)
            pe.wait_ge(S["setE"], 1)
            for j in range((NWIN + 3) // 4):
                w0, n = 4 * j, min(4, NWIN - 4 * j)
                if j >= 4:
                    pe.wait_ge(S["pr1"], j - 3)
                for v in range(n):
                    last = T.matmul(bank[:, 4 + j % 4, v * 128:(v + 1) * 128], hT[:, (w0 + v) * WS:(w0 + v) * WS + 128], w1aT[0:D, :],
                                    start=(v == 0), stop=True, skip_group_check=True)
                last.then_inc(S["proj"], 1)
            pe.wait_ge(S["setE"], 2)
            pe.wait_ge(S["const"], 2)

            def spread(g, u, load_count):
                pe.wait_ge(s_ea[u], load_count)
                if not isinstance(g, int) or g >= 1:
                    pe.wait_ge(S["Te"], g)
                pe.sem_inc(S["gate"], 1)
                for j in range(4):
                    last = T.transpose(pT[:, j * 128:(j + 1) * 128], ea[:, u, 2 * j:2 * j + 2, :].rearrange("p k f -> p (k f)"), I[:])
                last.then_inc(S["T"], 1)
                if not isinstance(g, int) or g >= 1:
                    pe.wait_ge(S["oh"], g)
                for par in range(2):
                    last = T.matmul(pR[:, par, :], ident_b[:, bass.ds(g, 1)].to_broadcast((128, 128)),
                                    rel[:, par, :, :].rearrange("p j e -> p (j e)"), start=True, stop=True)
                last.then_inc(S["Rb"], 1)

            def group(g, u, first, nxt, ranks):
                w = pe.value_load(win[0:1, bass.ds(g, 1)], min_val=0, max_val=NWIN - 1)
                if nxt is not None:
                    spread(g + 1, 1 - u, nxt)
                for par in range(2):
                    if par == 0:
                        pe.wait_ge(S["Te"], g + 1)
                        pe.wait_ge(S["oh"], g + 1)
                    if not first:
                        pe.wait_ge(S["rl"], g * 2 + par - 1)
                    T.matmul(pH[:, par, :], we2T[par * D:(par + 1) * D, :], eaT[par * D:(par + 1) * D, u, :], start=True, stop=False)
                    for c in range(3):
                        last = T.matmul(pH[:, par, :], pwin[:, bass.ds(w, 1), c, :].rearrange("p a h -> p (a h)"), oh[:, u, par, :],
                                        start=False, stop=(c == 2))
                    last.then_inc(S["H"], 1)
                if u == 0:
                    pe.wait_ge(S["rc"], ranks + 1)
                    T.matmul(RANK, below[:], rowcnt[:], start=False, stop=True, skip_group_check=True).then_inc(S["rk"], 1)
                else:
                    pe.wait_ge(S["pair"], ranks * PAIR_STEPS + 3)
                    T.matmul(RANK, not_below[:], rowcnt[:], start=False, stop=True, skip_group_check=True).then_inc(S["rkd"], 1)
                for par in range(2):
                    pe.wait_ge(S["rl"], g * 2 + par + 1)
                    if par == 0 and not first:
                        pe.wait_ge(S["r1"], g)
                    for j in range(4):
                        k = 2 * j + par
                        last = T.matmul(pM[:, k * D:(k + 1) * D], rT[:, par, j * 128:(j + 1) * 128], w1bT[:],
                                        start=(par == 0 and j == 0), stop=True, skip_group_check=True)
                    last.then_inc(S["M"], 1)

            def sum_block(n, v, c, acc, evacuated):
                pe.wait_ge(S["oh2"], n + 1)
                if evacuated is not None:
                    pe.wait_ge(S["ae"], evacuated)
                for t in range(c):
                    last = T.matmul(acc, oh2[:, v, t, :], rows[:, v, t, 0:AW], start=(t == 0), stop=(t == c - 1), skip_group_check=True)
                last.then_inc(S["ag"], 1)

            def pair(i, first=False, last=False, blocks=False, first_blocks=False):
                group(i * 2, 0, first, i * 16 + 16 if not last else 16 * (NP + 1), ranks=i)
                n = (i - P1) * BPP
                if blocks:
                    sum_block(n, 0, C1, acc1(0), None if first_blocks else (i - P1) * 2)
                    sum_block(n + 1, 1, C1, acc1(1), None)
                group(i * 2 + 1, 1, False, None if last else i * 16 + 32, ranks=i)
                if blocks:
                    sum_block(n + 2, 2, C1, acc1(0), (i - P1) * 2 + 1)

            def ranks_from(ph):
                T.matmul(RANK, ones_row[:], base[:, ph, :], start=True, stop=True, skip_group_check=True)

            pe.wait_ge(S["plo"], (NWIN + 3) // 4)
            ranks_from(0)
            spread(0, 0, 16)
            pair(0, first=True)
            with pe.Fori(1, P1) as i:
                pair(i)
            pe.wait_ge(S["rkf"], 1)
            ranks_from(1)
            pair(P1, blocks=True, first_blocks=True)
            with pe.Fori(P1 + 1, NP - 1) as i:
                pair(i, blocks=True)
            pair(NP - 1, last=True, blocks=True)
            n1 = BPP * (NP - P1)
            for v in range(NB - n1):
                sum_block(n1 + v, v, C1, acc1(0), 2 * (NP - P1) + v)

            def node(j, n, q, b0):
                c = n * BN
                pe.wait_ge(q["cat"], j + 1)
                pe.wait_ge(q["hc"], j + 1)
                pe.sem_inc(S["gate"], 1)
                for v in range(n):
                    last = T.transpose(bank[:, 0, v * BN:(v + 1) * BN], cat[:, v, :], I[0:BN, 0:BN])
                last.then_inc(q["catT"], 1)
                pe.wait_ge(q["catE"], j + 1)
                T.matmul(bank[:, 1, 0:c], w2aT[:], catT[:, 0:c], start=True, stop=True).then_inc(q["z1"], 1)
                pe.wait_ge(q["z1e"], j + 1)
                T.matmul(bank[0:D, 2, 0:c], w2bT[:], z1T[:, 0:c], start=True, stop=True).then_inc(q["z"], 1)
                pe.wait_ge(q["ze"], j + 1)
                for v in range(n):
                    T.matmul(bank[0:BN, 3, v * D:(v + 1) * D], zT[:, v * BN:(v + 1) * BN], wrzT[:], start=(v == 0), stop=False, skip_group_check=True)
                    last = T.matmul(bank[0:BN, 3, v * D:(v + 1) * D], catT[0:D, v * BN:(v + 1) * BN], wrhT[:], start=False, stop=True, skip_group_check=True)
                last.then_inc(q["o"], 1)

            def batch(j, n):
                for v in range(n):
                    if v == 0:
                        if isinstance(j, int) and j == 0:
                            pe.wait_ge(S["ae"], 2 * (NP - P1) + NB - BPP * (NP - P1))
                        else:
                            pe.wait_ge(S["batch"], j * BATCH_STEPS - MEAN_STEPS)
                    sum_block(j * 4 + NB + v, v, C2, acc2(v), None)

            batch(0, 4)
            with pe.Fori(1, NJ - 1) as j:
                batch(j, 4)
                node(j - 1, 4, NODE, (j - 1) * 4)
            batch(NJ - 1, batches[-1][1])
            node(NJ - 2, 4, NODE, (NJ - 2) * 4)
            node(NJ - 1, batches[-1][1], NODE, (NJ - 1) * 4)

            pe.wait_ge(S["flag"], 1)
            is_bad = pe.value_load(flag[0:1, 0:1], min_val=0, max_val=1)
            with pe.If(is_bad > 0):
                for k in range(K):
                    last = T.transpose(bank[:, 0, k * NG:(k + 1) * NG], idx_f[:, 1, :].rearrange("g (p k) -> g k p", k=K)[:, k, :], I[0:NG, 0:NG])
                last.then_inc(L["dT"], 1)
                pe.wait_ge(L["dTe"], 1)
                for b in range(NB):
                    if b >= 2:
                        pe.wait_ge(L["pje"], b - 1)
                    T.matmul(bank[0:BN, b % 2, 0:HID], hT[:, b * BN:(b + 1) * BN], w1aT[0:D, :], start=True, stop=True).then_inc(L["pj"], 1)
                pe.wait_ge(L["pje"], NB)

                def slow_group(g, u, loads, first):
                    pe.wait_ge(l_ea[u], loads)
                    pe.sem_inc(S["gate"], 1)
                    for k in range(K):
                        t = g * K + k
                        T.transpose(bank[0:D, 0, 0:128], ea[:, u, k, :], I[:]).then_inc(L["eT"], 1)
                        pe.wait_ge(l_g[k], g * 16 + 16)
                        T.matmul(bank[:, 1, 0:128], pg[:, k, :], I[:], start=True, stop=False)
                        pe.wait_ge(L["eTe"], t + 1)
                        T.matmul(bank[:, 1, 0:128], we2T[0:D, :], s_eaT, start=False, stop=True).then_inc(L["H"], 1)
                        pe.wait_ge(L["r"], t + 1)
                        T.matmul(bank[:, 2, 0:D], s_rT, w1bT[:], start=True, stop=True).then_inc(L["M"], 1)
                        pe.wait_ge(L["Me"], t + 1)
                        for b in range(NB):
                            last = T.matmul(slow_acc(b), s_onehot[:, b, :], s_msg[:], start=(first and k == 0 and b % PER_BANK == 0),
                                            stop=False, skip_group_check=True)
                        last.then_inc(L["used"], 1)

                slow_group(0, 0, 16, True)
                slow_group(1, 1, 16, False)
                with pe.Fori(1, NP - 1) as i:
                    slow_group(i * 2, 0, i * 16 + 16, False)
                    slow_group(i * 2 + 1, 1, i * 16 + 16, False)
                slow_group(NG - 2, 0, 16 * NP, False)
                slow_group(NG - 1, 1, 16 * (NP + 1), False)
                for j, (b0, n) in enumerate(batches):
                    node(j, n, n_sem, b0)
            pe.sem_inc(S["gate"], 1)


_INS = ['x', 'src', 'dst', 'edge_attr_64'] + ['L0_gnn_' + w for w in ('W1a', 'b1a', 'W1b', 'b1b', 'W2a', 'b2a', 'W2b', 'b2b', 'Wr', 'br')]


def kernel(**inputs):
    import numpy as np
    import concourse.bacc as bacc
    from concourse.bass_utils import run_bass_kernel_spmd
    nc = bacc.Bacc("TRN2", target_bir_lowering=False, num_devices=1)
    arrays, args = {}, []
    for name in _INS:
        a = np.ascontiguousarray(inputs[name])
        arrays[f"in_{name}"] = a
        args.append(nc.dram_tensor(f"in_{name}", a.shape, mybir.dt.from_np(a.dtype), kind="ExternalInput").ap())
    args.append(nc.dram_tensor("out_0", inputs['x'].shape, mybir.dt.float32, kind="ExternalOutput").ap())
    gnn_layer(nc, *args)
    r = run_bass_kernel_spmd(nc, [arrays], core_ids=[0])
    return r.results[0]["out_0"]
```

```python
import math
from contextlib import ExitStack

import concourse.bass as bass
from concourse import mybir



def gnn_layer(nc, x, src, dst, edge_attr, W1a, b1a, W1b, b1b, W2a, b2a, W2b, b2b, Wr, br, out):
    f32, i32, bf16 = mybir.dt.float32, mybir.dt.int32, mybir.dt.bfloat16
    ALU, ACT, AX = mybir.AluOpType, mybir.ActivationFunctionType, mybir.AxisListType

    N, D = x.shape
    E = src.shape[0]
    HID = W1a.shape[0]
    NB = 25
    BN = N // NB
    K = 8
    GE = 128 * K
    NG = (E + GE - 1) // GE
    NP = NG // 2
    PK = 2 * K
    LAST = E - (NG - 1) * GE
    LP, LR = LAST // K, LAST % K
    WS = 64
    NWB = ((N - 1) // WS + 4) // 4
    NWIN = 4 * NWB
    WC = 3 * WS + 128
    HC = (NWB - 1) * 4 * WS + WC
    WB0 = 2
    EPS = 1e-5
    MAGIC = 1.5 * 2 ** 23
    BIG = float(2 ** 18)

    P2, P3 = 7, 19
    STARTS = (0, P2, P3, NP)
    S1, S2 = 6, 4
    WP = NWB - WB0
    HP = 4
    Q1 = WP + HP

    def capacity(ph):
        edges = min(E, STARTS[ph + 1] * 2 * GE) - STARTS[ph] * 2 * GE
        mean = edges * (E - N) / E / NB
        return math.ceil((mean + BN + 4 * math.sqrt(mean)) / 128)

    C = [capacity(ph) for ph in range(3)]
    FILLS = [None, (P2 - 1, 4), (Q1 - 1 - P2, 2)]
    FT = [C[0]] + [-(-NB * C[ph] // (FILLS[ph][0] * FILLS[ph][1])) for ph in (1, 2)]
    ROOM = [NB * C[0]] + [FILLS[ph][0] * FILLS[ph][1] * FT[ph] for ph in (1, 2)]
    BEGIN = [sum(ROOM[:ph]) * 128 for ph in range(3)]
    SLOTS = sum(ROOM) * 128
    RW = 3 * D + 2
    AW = 3 * D + 1
    MID, LOW, HIGH, MARK = 0, D, 2 * D, 3 * D
    NQ = NB + 1
    TB = 12
    RT = max(S1 * C[0], S2 * C[1], TB * C[2])
    OT = max(S1 * C[0], S2 * C[1], 8 * C[2])

    with ExitStack() as ctx:
        def sb(name, shape, dt=f32):
            return ctx.enter_context(nc.sbuf_tensor(name, shape, dt))

        def sem(name):
            return ctx.enter_context(nc.semaphore(name))

        ident = sb("ident", [128, 128])
        ident_b = sb("ident_b", [128, 128], bf16)
        below = sb("below", [128, 128], bf16)
        not_below = sb("not_below", [128, 128], bf16)
        ones_row = sb("ones_row", [1, 128])
        ones_b = sb("ones_b", [96, 128], bf16)
        place = sb("place", [128, 1])
        rec_mark = sb("rec_mark", [128, 1])
        marks = [sb(f"marks{ph}", [128, BN, c], bf16) for ph, c in enumerate(C)]
        bucket_row = sb("bucket_row", [128, NQ])
        restart = sb("restart", [128, NQ, PK])
        base = sb("base", [1, 3, NQ])
        reach = sb("reach", [NG, 1])
        w1a_in = sb("w1a_in", [HID, 2 * D])
        w1b_in = sb("w1b_in", [D, HID])
        w2a_in = sb("w2a_in", [HID, 2 * D])
        w2b_in = sb("w2b_in", [D, HID])
        wr_in = sb("wr_in", [D, 2 * D])
        w1aT = sb("w1aT", [2 * D, HID])
        we2T = sb("we2T", [2 * D, HID])
        w1bT = sb("w1bT", [HID, D])
        w2aT = sb("w2aT", [2 * D, HID])
        wrzT = sb("wrzT", [D, D])
        wrhT = sb("wrhT", [D, D])
        w2r = sb("w2r", [HID, D])
        b1b_all = sb("b1b_all", [128, D])
        b1b_p = sb("b1b_p", [96, 3, D])
        b1b_b = sb("b1b_b", [96, 2, D], bf16)
        b1b_rows = sb("b1b_rows", [96, K, D], bf16)
        br_row = sb("br_row", [1, D])
        bias_row = sb("bias_row", [1, D])
        b1a_col = sb("b1a_col", [HID, 1])
        b2a_col = sb("b2a_col", [HID, 1])
        b2b_col = sb("b2b_col", [D, 1])
        zeros = sb("zeros", [128, max(FT) * RW], bf16)

        xs = sb("xs", [BN, NB, D])
        warm = sb("warm", [1, 1])
        h = sb("h", [BN, NB, D])
        xc = sb("xc", [BN, NB, D])
        ot = sb("ot", [BN, NB, D])
        stat = sb("stat", [BN, 4, NB])
        catT = sb("catT", [2 * D, HC])
        hT = catT[0:D]
        hTw = sb("hTw", [D, WC])
        pwin = sb("pwin", [128, NWIN, 3, HID], bf16)
        rest = sb("rest", [128, 512])
        sums = sb("sums", [BN, NB, D + 1])
        cnt = sb("cnt", [BN, 3, 4])
        mean = sb("mean", [BN, 4, D])
        cat = sb("cat", [BN, 2, 4, 2 * D])
        z1T = sb("z1T", [HID, 4 * BN])

        idx_i = sb("idx_i", [NG, 2, GE], i32)
        idx_f = sb("idx_f", [NG, GE])
        rel = sb("rel", [128, 2, 4, 128], bf16)
        wstat = sb("wstat", [NG, 4])
        win = sb("win", [1, NG], i32)
        bad = sb("bad", [1, 6])
        region_fill = sb("region_fill", [1, NQ])
        flag = sb("flag", [1, 1], i32)
        srcL = sb("srcL", [128, NG, K])
        srcq = sb("srcq", [128, NG, K])
        mark = sb("mark", [128, NG, K])
        limit = sb("limit", [128, NG, K])
        eq = sb("eq", [128, NQ, PK])
        incl = sb("incl", [128, NQ, PK])
        slot_t = sb("slot_t", [128, NQ, PK])
        rowcnt = sb("rowcnt", [128, NQ], bf16)
        pos = sb("pos", [128, 3, PK])
        pos_i = sb("pos_i", [128, 2, K], i32)
        ea = sb("ea", [128, 2, K, D])
        eaT = sb("eaT", [2 * D, 2, 512])
        oh = sb("oh", [128, 2, 2, 512], bf16)
        rT = sb("rT", [HID, 2, 512])
        r1 = sb("r1", [128, 2, K, D])
        pay = sb("pay", [128, 2, K, RW], bf16)
        rows = sb("rows", [128, RT, RW], bf16)
        rmark = sb("rmark", [128, RT], bf16)
        oh2 = sb("oh2", [128, OT * BN], bf16)
        slots_dram = nc.dram_tensor("slots_dram", (SLOTS, RW), bf16, kind="Internal").ap()
        proj_dram = nc.dram_tensor("proj_dram", (N, HID), f32, kind="Internal").ap()

        old = pwin[:].rearrange("p w c h -> p (w c h)").bitcast(f32)
        node_row = old[:, 0:NB * BN]
        s_onehot = old[:, NB * BN:2 * NB * BN].rearrange("p (b n) -> p b n", n=BN)
        o = 2 * NB * BN
        pg = old[:, o:o + K * HID].rearrange("p (k h) -> p k h", h=HID)
        o += K * HID
        s_proj = old[0:BN, o:o + 2 * HID].rearrange("p (a h) -> p a h", h=HID)
        o += 2 * HID
        s_msg = old[:, o:o + D + 1]
        o += D + 2
        s_eaT = old[0:D, o:o + 128]
        o += 128
        s_rT = old[:, o:o + 128]
        o += 128
        s_cnt = old[0:BN, o:o + 3 * NB].rearrange("p (a b) -> p a b", b=NB)
        ints = rows[:].rearrange("p t w -> p (t w)").bitcast(i32)
        dstL = ints[:, 0:NG * K].rearrange("p (g k) -> p g k", k=K)
        dst_now = ints[:, NG * K:NG * K + K]

        bank = ctx.enter_context(nc.psum_tensor("bank", [128, 8, 512], f32))
        pT, pM, pR = bank[:, 0, :], bank[:, 1, :], bank[:, 2:4, :]
        pH = bank[:, 4:6, :]
        RANK = bank[:, 7, 0:NQ]
        SPARE = 6
        PER_BANK = 7

        def acc(v, b=SPARE):
            return bank[0:BN, b, v * 256:v * 256 + AW]

        def slow_acc(b):
            c = (b % PER_BANK) * (D + 1)
            return bank[0:BN, 4 + b // PER_BANK, c:c + D + 1]

        names = dict(
            w_in="weights_loaded", pad="pads_set", id="identity_made",
            const="constants_made", zero="zeros_made", fill1="regions_1_cleared", v="vector_step",
            xc="x_centered", sq="squares", var="variance_made", sd="deviation", rx="relu_of_centered", h="h_made", fsrc="src_as_float", fdst="dst_as_float", tmark="tail_marks_taken",
            setT="setup_transposed", setE="weights_evacuated", srcE="src_prepared", setW="weights_combined", setWe="combined_evacuated",
            hTt="h_transposed", hTa="hT_evacuated_by_scalar", hTd="hT_evacuated_by_vector", hw="window_hT_taken",
            proj="windows_made", phi="windows_high", pr1="windows_rest", pmid="windows_middle", plo="windows_low",
            wready="windows_chosen", xh="h_part_made", xhe="h_part_added",
            T="edges_transposed", Te="edges_T_evacuated", Rb="rel_spread", oh="onehot_made", H="hidden_made", rl="hidden_relu",
            M="messages_made", hi="messages_high", r1="messages_rest", mid="messages_middle", payd="rows_ready", rc="row_counts",
            rk="ranks_made", rkd="ranks_moved_on", rkf="ranks_checked", hots="marks_taken", oh2="sum_onehot_made", ag="block_summed",
            ae="block_sums_read", cat="mean_made", catT="mean_transposed", catE="cat_evacuated", z1="z1_made", z1e="z1_relu",
            o="out_made", oe="out_added", out="out_stored", flag="flag_set", gate="passed", pair="rank_step", tail="mean_step")
        S = {k: sem(v) for k, v in names.items()}
        s_x = [sem("x_loaded_0"), sem("x_loaded_1")]
        s_idx = [sem("src_loaded"), sem("dst_loaded")]
        s_ea = [sem("edges_loaded_0"), sem("edges_loaded_1")]
        s_fill = [sem("regions_2_cleared"), sem("regions_3_cleared")]
        s_sc = [sem("rows_scattered_0"), sem("rows_scattered_1")]
        s_row = [sem(f"region_loaded_{v}") for v in range(TB)]
        s_names = ("pj", "pje", "eT", "eTe", "H", "r", "M", "Me", "used", "stage", "iota", "dT", "dTe")
        L = {k: sem("slow_" + k) for k in s_names}
        l_pst = [sem("slow_projection_stored_0"), sem("slow_projection_stored_1")]
        l_g = [sem(f"slow_rows_gathered_{k}") for k in range(K)]
        l_ea = [sem("slow_edges_loaded_0"), sem("slow_edges_loaded_1")]
        NODE = {k: S[k] for k in ("cat", "catT", "catE", "z1", "z1e", "o", "oe")}
        AGAIN = {k: sem("again_" + k) for k in NODE}
        NWT = 11
        PAIR_STEPS = 7

        def edges_of(g):
            return edge_attr[bass.ds(g * GE, GE), :].rearrange("(p k) f -> p k f", k=K)

        def last_edges(sp, done):
            g0 = (NG - 1) * GE
            sp.dma_start(ea[0:LP, 1, :, :], edge_attr[g0:g0 + LP * K, :].rearrange("(p k) f -> p k f", k=K)).then_inc(done, 16)
            sp.dma_start(ea[LP:LP + 1, 1, 0:LR, :], edge_attr[g0 + LP * K:E, :].rearrange("(p k) f -> p k f", k=LR)).then_inc(done, 16)

        def region(ph, b):
            return slots_dram[bass.ds(b * (C[ph] * 128) + BEGIN[ph], C[ph] * 128), :].rearrange("(p t) w -> p t w", t=C[ph])

        PARTS = ((0, 8), (8, NB))
        batches = [(4 * j, min(4, NB - 4 * j)) for j in range((NB + 3) // 4)]
        NJ = len(batches)

        def hT_bank(j):
            return 4 + j if j < 2 else SPARE

        assert NJ == 7

        def is_early(i):
            return isinstance(i, int) and i < 2

        h_parts = [(a * 7, min(7, NB - a * 7)) for a in range(HP)]
        assert sum(n for _, n in h_parts) == NB

        N1, N2 = P3 - Q1, NP - P3 - 1
        assert P2 < WP and 0 < NB - S1 * N1 <= 1 and 0 < NB - S2 * N2 <= 1
        R1, R2 = S1 // 2, S2 // 2
        USES = [[0] * TB, [N1 * (v < S1) + (v == 0) for v in range(TB)], None]
        USES[2] = [USES[1][v] + N2 * (v < S2) + (v == 0) for v in range(TB)]

        def one_hot_rows(ph, v, m=1):
            c = C[ph]
            return oh2[:, v * c * BN:(v + m) * c * BN].rearrange("p (v n t) -> p v n t", n=BN, t=c)

        def row_tiles(ph, v, m=1):
            return rows[:, v * C[ph]:(v + m) * C[ph], :]

        block = ctx.enter_context(nc.Block())

        @block.sync
        def _(sp):
            x_v = x.rearrange("(b p) f -> p b f", p=BN)

            def load_x(part):
                b0, b1 = PARTS[part]
                sp.dma_start(xs[:, b0:b1, :], x_v[:, b0:b1, :]).then_inc(s_x[part], 16)

            load_x(0)
            sp.wait_ge(S["pad"], 1)
            for n, a in ((1, dst), (0, src)):
                sp.dma_start(idx_i[0:NG - 1, n, :], a[0:(NG - 1) * GE].rearrange("(g e) -> g e", e=GE)).then_inc(s_idx[n], 16)
                sp.dma_start(idx_i[NG - 1:NG, n, 0:LAST], a[(NG - 1) * GE:E].rearrange("(g e) -> g e", g=1)).then_inc(s_idx[n], 16)
            load_x(1)
            for t, a in ((w1a_in, W1a), (w1b_in, W1b), (w2a_in, W2a), (w2b_in, W2b), (wr_in, Wr)):
                sp.dma_start(t[:], a).then_inc(S["w_in"], 16)
            for t, a, n in ((b1b_all[:], b1b, 128), (b1b_p[:, 0, :], b1b, 96), (br_row[:], br, 1)):
                sp.dma_start(t, a.rearrange("(o n) -> o n", o=1).to_broadcast((n, D))).then_inc(S["w_in"], 16)
            for t, a in ((b1a_col, b1a), (b2a_col, b2a), (b2b_col, b2b)):
                sp.dma_start(t[:], a.rearrange("(n o) -> n o", o=1)).then_inc(S["w_in"], 16)
            for g in range(2):
                sp.dma_start(ea[:, g, :, :], edges_of(g)).then_inc(s_ea[g], 16)
            sp.wait_ge(S["zero"], 1)
            for b in range(NB):
                sp.dma_start(region(0, b).rearrange("p t w -> p (t w)"), zeros[:, 0:C[0] * RW]).then_inc(S["fill1"], 16)

            def load(g, u):
                sp.wait_ge(S["T"], g - 1)
                sp.dma_start(ea[:, u, :, :], edges_of(g)).then_inc(s_ea[u], 16)

            load(2, 0)
            load(3, 1)

            def clear(ph, n, a):
                per = FILLS[ph][1]
                first = n * (per * FT[ph] * 128) + (BEGIN[ph] + a * FT[ph] * 128)
                sp.dma_start(slots_dram[bass.ds(first, FT[ph] * 128), :].rearrange("(p t) w -> p (t w)", p=128),
                             zeros[:, 0:FT[ph] * RW]).then_inc(s_fill[ph - 1], 16)

            with sp.Fori(1, P2) as i:
                load(i * 2 + 2, 0)
                clear(1, i - 1, 0)
                clear(1, i - 1, 1)
                load(i * 2 + 3, 1)
                clear(1, i - 1, 2)
                clear(1, i - 1, 3)

            def load_blocks(ph, b, n, summed=None):
                for v in range(n):
                    if summed is not None:
                        sp.wait_ge(S["ag"], summed + v)
                    sp.dma_start(row_tiles(ph, v), region(ph, b + v)).then_inc(s_row[v], 16)

            with sp.Fori(P2, Q1 - 1) as i:
                load(i * 2 + 2, 0)
                clear(2, i - P2, 0)
                load(i * 2 + 3, 1)
                clear(2, i - P2, 1)
            load(Q1 * 2, 0)
            load(Q1 * 2 + 1, 1)
            for u in range(2):
                sp.wait_ge(s_sc[u], 16 * K * P2)
            load_blocks(0, 0, S1)
            load(Q1 * 2 + 2, 0)
            load(Q1 * 2 + 3, 1)
            with sp.Fori(Q1 + 1, P3) as i:
                load(i * 2 + 2, 0)
                load_blocks(0, (i - Q1) * S1, S1, (i - Q1 - 1) * S1 + 1)
                load(i * 2 + 3, 1)
            load(P3 * 2 + 2, 0)
            load_blocks(0, S1 * N1, 1, S1 * (N1 - 1) + 1)
            load(P3 * 2 + 3, 1)
            for u in range(2):
                sp.wait_ge(s_sc[u], 16 * K * P3)
            sp.wait_ge(S["ag"], NB)
            load_blocks(1, 0, S2)
            load(P3 * 2 + 4, 0)
            load(P3 * 2 + 5, 1)
            with sp.Fori(P3 + 2, NP - 2) as i:
                load(i * 2 + 2, 0)
                load_blocks(1, (i - P3 - 1) * S2, S2, (i - P3 - 2) * S2 + NB + 1)
                load(i * 2 + 3, 1)
            load(NG - 2, 0)
            load_blocks(1, (NP - 2 - P3 - 1) * S2, S2, (NP - 2 - P3 - 2) * S2 + NB + 1)
            sp.wait_ge(S["T"], NG - 2)
            last_edges(sp, s_ea[1])
            load_blocks(1, (NP - 1 - P3 - 1) * S2, S2, (NP - 1 - P3 - 2) * S2 + NB + 1)
            load_blocks(1, S2 * N2, 1, NB + S2 * (N2 - 1) + 1)
            sp.wait_ge(S["ag"], 2 * NB)
            for u in range(2):
                sp.wait_ge(s_sc[u], 16 * K * NP)
            for b in range(NB):
                if b >= TB:
                    sp.wait_ge(S["ag"], 2 * NB + b - TB + 1)
                sp.dma_start(row_tiles(2, b % TB), region(2, b)).then_inc(s_row[b % TB], 16)
            half = 20
            sp.wait_ge(S["oe"], half // 4)
            o_v, t_v = out.rearrange("(b p) f -> p b f", p=BN), ot
            sp.dma_start(o_v[:, 0:half, :], t_v[:, 0:half, :]).then_inc(S["out"], 16)
            sp.wait_ge(S["oe"], NJ)
            sp.dma_start(o_v[:, half:NB, :], t_v[:, half:NB, :]).then_inc(S["out"], 16)
            sp.wait_ge(S["out"], 32)
            sp.wait_ge(S["flag"], 1)
            is_bad = sp.value_load(flag[0:1, 0:1], min_val=0, max_val=1)
            with sp.If(is_bad > 0):
                for b in range(NB):
                    sp.wait_ge(L["pje"], b + 1)
                    sp.dma_start(proj_dram[b * BN:(b + 1) * BN, :], s_proj[:, b % 2, :]).then_inc(l_pst[b % 2], 16)
                for g in range(2):
                    sp.dma_start(ea[:, g, :, :], edges_of(g)).then_inc(l_ea[g], 16)

                def slow_load(g, u):
                    sp.wait_ge(L["used"], g * K - K)
                    sp.dma_start(ea[:, u, :, :], edges_of(g)).then_inc(l_ea[u], 16)

                with sp.Fori(1, NP - 1) as i:
                    slow_load(i * 2, 0)
                    slow_load(i * 2 + 1, 1)
                slow_load(NG - 2, 0)
                sp.wait_ge(L["used"], (NG - 2) * K)
                last_edges(sp, l_ea[1])
                sp.wait_ge(AGAIN["oe"], NJ)
                sp.dma_start(o_v, t_v[:]).then_inc(S["out"], 16)
                sp.wait_ge(S["out"], 48)
            sp.sem_inc(S["gate"], 1)

        @block.gpsimd
        def _(pool):
            G = nc.gpsimd
            q0 = (NG - 1) // 32 * 32
            G.memset(idx_i[q0:NG, 0, LAST:GE], NB * BN)
            G.memset(idx_i[q0:NG, 1, LAST:GE], N - 1).then_inc(S["pad"], 1)
            pool.wait_ge(S["pad"], 1)
            G.memset(ident[:], 0.0).then_inc(S["id"], 1)
            G.memset(zeros[:], 0.0).then_inc(S["zero"], 1)
            pool.wait_ge(S["id"], 1)
            G.affine_select(out=ident[:], in_=ident[:], compare_op=ALU.not_equal, fill=1.0, base=0,
                            pattern=[[-1, 128]], channel_multiplier=1).then_inc(S["id"], 1)

            def count(t, pattern, first, down):
                return G.iota(t, pattern=pattern, base=first, channel_multiplier=down, allow_small_or_imprecise_dtypes=True)

            G.memset(rel[:], 0.0)
            G.memset(hT[:, N:HC], 0.0)
            count(reach[:], [[0, 1]], 4 * WB0 - 3, 2)
            count(place[:], [[0, 1]], 0, 1).then_inc(S["const"], 1)
            pool.wait_ge(s_idx[0], 32)
            G.tensor_copy(idx_f[:], idx_i[:, 0, :]).then_inc(S["fsrc"], 1)
            G.memset(below[:], 1.0)
            G.memset(not_below[:], 1.0)
            G.memset(restart[:], 1.0).then_inc(S["id"], 1)
            pool.wait_ge(S["id"], 3)
            G.affine_select(out=below[:], in_=below[:], compare_op=ALU.is_gt, fill=0.0, base=0,
                            pattern=[[1, 128]], channel_multiplier=-1)
            G.affine_select(out=not_below[:], in_=not_below[:], compare_op=ALU.is_ge, fill=0.0, base=0,
                            pattern=[[-1, 128]], channel_multiplier=1)
            G.memset(restart[:, :, 0:1], 0.0)
            count(bucket_row[:], [[1, NQ]], 0, 0)
            for ph in range(3):
                count(base[:, ph, 0:NB], [[C[ph] * 128, NB]], BEGIN[ph] - 1, 0)
            G.memset(base[:, :, NB:NQ], BIG)
            G.memset(pay[:, :, :, AW:RW], 0.0)
            G.memset(b1b_rows[:], 0.0)
            G.memset(ones_b[:], 1.0)
            G.memset(ones_row[:], 1.0)
            G.tensor_copy(ident_b[:], ident[:]).then_inc(S["const"], 1)
            count(rec_mark[:], [[0, 1]], 1, 1)
            G.memset(cat[:], 0.0)
            for ph in range(3):
                last = count(marks[ph][:], [[1, BN], [0, C[ph]]], 1, 0)
            last.then_inc(S["const"], 1)

            def scatter(i, u):
                pool.wait_ge(S["payd"], i * 2 + u + 1)
                pool.sem_inc(S["gate"], 1)
                for k in range(K):
                    pool.indirect_dma_start(out=slots_dram[:, :], out_offset=bass.IndirectOffsetOnAxis(ap=pos_i[:, u, k:k + 1], axis=0),
                                            in_=pay[:, u, k, :], in_offset=None, bounds_check=SLOTS - 1, oob_is_err=False
                                            ).then_inc(s_sc[u], 16)

            pool.wait_ge(S["fill1"], 16 * NB)
            with pool.Fori(0, P2) as i:
                scatter(i, 0)
                scatter(i, 1)
            for ph in (1, 2):
                pool.wait_ge(s_fill[ph - 1], 16 * FILLS[ph][0] * FILLS[ph][1])
                with pool.Fori(STARTS[ph], STARTS[ph + 1]) as i:
                    scatter(i, 0)
                    scatter(i, 1)

            pool.wait_ge(S["flag"], 1)
            is_bad = pool.value_load(flag[0:1, 0:1], min_val=0, max_val=1)
            with pool.If(is_bad > 0):
                G.tensor_copy(idx_f[:], idx_i[:, 1, :]).then_inc(S["fdst"], 1)
                pool.wait_ge(S["fdst"], 1)
                G.iota(node_row, pattern=[[1, NB * BN]], base=0, channel_multiplier=0,
                       allow_small_or_imprecise_dtypes=True).then_inc(L["iota"], 1)
                pool.wait_ge(l_pst[0], 16 * ((NB + 1) // 2))
                pool.wait_ge(l_pst[1], 16 * (NB // 2))
                with pool.Fori(0, NG) as g:
                    pool.wait_ge(L["stage"], g + 1)
                    pool.sem_inc(S["gate"], 1)
                    for k in range(K):
                        pool.indirect_dma_start(out=pg[:, k, :], out_offset=None, in_=proj_dram,
                                                in_offset=bass.IndirectOffsetOnAxis(ap=dst_now[:, k:k + 1], axis=0)
                                                ).then_inc(l_g[k], 16)
            pool.sem_inc(S["gate"], 1)

        @block.vector
        def _(dve):
            V = nc.vector
            done = [0]

            def link(ins):
                done[0] += 1
                ins.then_inc(S["v"], 1)
                dve.wait_ge(S["v"], done[0])

            def center(part):
                b0, b1 = PARTS[part]
                dve.wait_ge(s_x[part], 16)
                link(V.tensor_reduce(stat[:, 0, b0:b1], xs[:, b0:b1, :], axis=AX.X, op=ALU.add))
                link(V.tensor_scalar(stat[:, 0, b0:b1], stat[:, 0, b0:b1], 1.0 / D, None, ALU.mult))
                V.tensor_tensor(xc[:, b0:b1, :], xs[:, b0:b1, :], stat[:, 0, b0:b1].unsqueeze(2).to_broadcast((BN, b1 - b0, D)),
                                ALU.subtract).then_inc(S["xc"], 1)

            def variance(part):
                b0, b1 = PARTS[part]
                dve.wait_ge(S["sq"], part + 1)
                link(V.tensor_reduce(stat[:, 1, b0:b1], ot[:, b0:b1, :], axis=AX.X, op=ALU.add))
                V.tensor_scalar(stat[:, 1, b0:b1], stat[:, 1, b0:b1], 1.0 / D, EPS, ALU.mult, ALU.add).then_inc(S["var"], 1)

            def make_h(part):
                b0, b1 = PARTS[part]
                dve.wait_ge(S["sd"], part + 1)
                link(V.reciprocal(stat[:, 3, b0:b1], stat[:, 2, b0:b1]))
                dve.wait_ge(S["rx"], part + 1)
                V.tensor_tensor(h[:, b0:b1, :], xc[:, b0:b1, :], stat[:, 3, b0:b1].unsqueeze(2).to_broadcast((BN, b1 - b0, D)),
                                ALU.mult).then_inc(S["h"], 1)

            center(0)
            dstI = idx_i[:, 1, :]
            dve.wait_ge(s_idx[1], 32)
            link(V.tensor_reduce(wstat[:, 0:1], dstI, axis=AX.X, op=ALU.min))
            variance(0)
            link(V.tensor_scalar(wstat[:, 2:3], wstat[:, 0:1], 1.0 / WS, 0.5 / WS - 0.5, ALU.mult, ALU.add))
            link(V.tensor_scalar(wstat[:, 2:3], wstat[:, 2:3], MAGIC, -MAGIC, ALU.add, ALU.add))
            dve.wait_ge(S["const"], 1)
            link(V.tensor_tensor(wstat[:, 2:3], wstat[:, 2:3], reach[:], ALU.min))
            link(V.tensor_scalar(wstat[:, 0:1], wstat[:, 2:3], float(WS), None, ALU.mult))
            make_h(0)
            V.tensor_scalar(rel[0:NG].rearrange("g r j p -> g p j r"), dstI.rearrange("g (p j r) -> g p j r", j=4, r=2),
                            wstat[:, 0:1], None, ALU.subtract)
            link(V.tensor_reduce(wstat[:, 1:2], dstI, axis=AX.X, op=ALU.max))
            V.tensor_tensor(wstat[:, 3:4], wstat[:, 1:2], wstat[:, 0:1], ALU.subtract).then_inc(S["wready"], 1)
            center(1)
            b0, n = batches[1]
            dve.wait_ge(S["hTt"], 2)
            V.tensor_copy(hT[:, b0 * BN:(b0 + n) * BN], bank[0:D, hT_bank(1), 0:n * BN]).then_inc(S["hTd"], 1)
            dve.wait_ge(S["setT"], 2)
            link(V.tensor_copy(srcL[:].rearrange("p g k -> p k g"), bank[:, 2, 0:K * NG].rearrange("p (k g) -> p k g", g=NG)))
            V.tensor_reduce(bad[:, 0:1], bank[0:1, 3, 128:128 + NG], axis=AX.X, op=ALU.max)
            V.tensor_copy(win[:], bank[0:1, 3, 0:NG]).then_inc(S["srcE"], 1)

            def window_rest(j):
                dve.wait_ge(S["phi"], j + 1)
                V.tensor_tensor(rest[:].rearrange("p (w h) -> p w h", h=HID), bank[:, SPARE, :].rearrange("p (w h) -> p w h", h=HID),
                                pwin[:, bass.ds(j * 4, 4), 0, :], ALU.subtract).then_inc(S["pr1"], 1)

            def window_low(j):
                dve.wait_ge(S["pmid"], j + 1)
                V.tensor_tensor(pwin[:, bass.ds(j * 4, 4), 2, :], rest[:].rearrange("p (w h) -> p w h", h=HID),
                                pwin[:, bass.ds(j * 4, 4), 1, :], ALU.subtract).then_inc(S["plo"], 1)
                dve.wait_ge(S["plo"], j + 1)

            def onehot(g, u):
                dve.wait_ge(S["Rb"], g + 1)
                if not isinstance(g, int) or g >= 2:
                    dve.wait_ge(S["H"], (g - 1) * 2)
                V.tensor_scalar(oh[:, u, :, :], pR, place[:], None, ALU.is_equal).then_inc(S["oh"], 1)

            link(V.tensor_scalar(srcq[:], srcL[:], 1.0 / BN, 0.5 / BN - 0.5, ALU.mult, ALU.add))
            window_rest(0)
            link(V.tensor_scalar(srcq[:], srcq[:], MAGIC, -MAGIC, ALU.add, ALU.add))
            window_low(0)
            variance(1)
            window_rest(1)
            onehot(0, 0)
            window_low(1)
            make_h(1)
            dve.wait_ge(S["w_in"], 16 * NWT)
            dve.wait_ge(S["const"], 2)
            link(V.tensor_copy(b1b_b[:, 0, :], b1b_p[:, 0, :]))
            link(V.tensor_tensor(b1b_p[:, 1, :], b1b_p[:, 0, :], b1b_b[:, 0, :], ALU.subtract))
            link(V.tensor_copy(b1b_b[:, 1, :], b1b_p[:, 1, :]))
            link(V.tensor_tensor(b1b_p[:, 2, :], b1b_p[:, 1, :], b1b_b[:, 1, :], ALU.subtract))
            for part, a in ((0, b1b_b[0:1, 0, :]), (32, b1b_b[32:33, 1, :]), (64, b1b_p[64:65, 2, :])):
                last = V.tensor_copy(b1b_rows[part:part + 1, :, :], a.unsqueeze(1).to_broadcast((1, K, D)))
            last.then_inc(S["srcE"], 1)

            def places():
                for ph in range(3):
                    g0, g1 = STARTS[ph] * 2, STARTS[ph + 1] * 2
                    V.tensor_scalar(limit[:, g0:g1, :], srcq[:, g0:g1, :], C[ph] * 128.0, C[ph] * 128 + BEGIN[ph] - 1.0, ALU.mult, ALU.add)
                link(V.scalar_tensor_tensor(mark[:], srcq[:], -float(BN), srcL[:], ALU.mult, ALU.add))
                link(V.tensor_scalar(mark[:], mark[:], 1.0, None, ALU.add))

            def chain(i, of, per):
                n = [0]

                def step(ins):
                    n[0] += 1
                    ins.then_inc(of, 1)
                    dve.wait_ge(of, i * per + n[0])

                return step

            def by_bucket(a):
                return a.unsqueeze(2).to_broadcast((128, NQ, PK))

            def ranks_a(i, step):
                if not isinstance(i, int) or i:
                    dve.wait_ge(S["payd"], i * 2)
                q = srcq[:, bass.ds(i * 2, 2), :].rearrange("p g k -> p (g k)")
                step(V.tensor_tensor(eq[:], q.unsqueeze(1).to_broadcast((128, NQ, PK)), by_bucket(bucket_row[:]), ALU.is_equal))
                flat = "p b k -> p (b k)"
                step(V.tensor_tensor_scan(incl[:].rearrange(flat), restart[:].rearrange(flat), eq[:].rearrange(flat), 0.0,
                                          ALU.mult, ALU.add))
                if not isinstance(i, int) or i:
                    dve.wait_ge(S["rkd"], i)
                V.tensor_copy(rowcnt[:], incl[:, :, PK - 1]).then_inc(S["rc"], 1)

            def ranks_b(i, step):
                dve.wait_ge(S["rk"], i + 1)
                step(V.tensor_tensor(slot_t[:], incl[:], by_bucket(RANK), ALU.add))
                step(V.tensor_tensor(slot_t[:], slot_t[:], eq[:], ALU.mult))
                step(V.tensor_reduce(pos[:, 0, :], slot_t[:].rearrange("p b k -> p k b"), axis=AX.X, op=ALU.add))
                lim = limit[:, bass.ds(i * 2, 2), :].rearrange("p g k -> p (g k)")
                step(V.tensor_tensor(pos[:, 1, :], pos[:, 0, :], lim, ALU.is_gt))
                step(V.scalar_tensor_tensor(pos[:, 2, :], pos[:, 1, :], BIG, pos[:, 0, :], ALU.mult, ALU.add))

            def payload(g, u):
                dve.wait_ge(S["hi"], g + 1)
                m = pM.rearrange("p (k f) -> p k f", f=D)
                V.tensor_tensor(r1[:, u, :, :], m, pay[:, u, :, HIGH:HIGH + D], ALU.subtract).then_inc(S["r1"], 1)
                V.tensor_copy(pos_i[:, u, :], pos[:, 2, u * K:(u + 1) * K])
                V.tensor_copy(pay[:, u, :, MARK], mark[:, bass.ds(g, 1), :].rearrange("p g k -> p (g k)"))
                dve.wait_ge(S["mid"], g + 1)
                V.tensor_tensor(pay[:, u, :, LOW:LOW + D], r1[:, u, :, :], pay[:, u, :, MID:MID + D], ALU.subtract).then_inc(S["payd"], 1)

            def onehots_of(ph, v, m, r):
                c = C[ph]
                n_t = (128, m, BN, c)
                V.tensor_tensor(one_hot_rows(ph, v, m), marks[ph][:].unsqueeze(1).to_broadcast(n_t),
                                rmark[:, r * c:(r + m) * c].rearrange("p (v t) -> p v t", t=c).unsqueeze(2).to_broadcast(n_t),
                                ALU.is_equal).then_inc(S["oh2"], m)

            def round_onehots(ph, use, vs, step):
                c, v0, m = C[ph], vs[0], len(vs)
                for v in vs:
                    dve.wait_ge(s_row[v], (use + USES[ph][v]) * 16)
                step(V.tensor_copy(rmark[:, v0 * c:(v0 + m) * c], rows[:, v0 * c:(v0 + m) * c, MARK]))
                onehots_of(ph, v0, m, v0)

            def take_sums(n, b, m):
                dve.wait_ge(S["ag"], n + m)
                a = bank[0:BN, SPARE, :].rearrange("p (v w) -> p v w", w=256)[:, 0:m, 0:AW]
                V.tensor_reduce(sums[:, bass.ds(b, m), 0:D], a[:, :, 0:3 * D].rearrange("p v (c f) -> p v f c", c=3), axis=AX.X, op=ALU.add)
                V.tensor_copy(sums[:, bass.ds(b, m), D], a[:, :, MARK]).then_inc(S["ae"], 1)

            def check_ranks(ph):
                dve.wait_ge(S["rkd"], STARTS[ph + 1])
                link(V.tensor_tensor(region_fill[:], RANK[0:1, :], base[:, ph, :], ALU.subtract))
                link(V.tensor_reduce(bad[:, 1 + ph:2 + ph], region_fill[:, 0:NB], axis=AX.X, op=ALU.max))
                V.tensor_scalar(bad[:, 1 + ph:2 + ph], bad[:, 1 + ph:2 + ph], C[ph] * 128 + 0.5, None, ALU.is_gt).then_inc(S["rkf"], 1)
                dve.wait_ge(S["rkf"], ph + 1)

            def add_h_part(a):
                b0, n = h_parts[a]
                dve.wait_ge(S["xh"], a + 1)
                V.tensor_tensor(xs[:, b0:b0 + n, :], xs[:, b0:b0 + n, :], bank[0:BN, SPARE, 0:n * D].rearrange("p (b f) -> p b f", f=D),
                                ALU.add).then_inc(S["xhe"], 1)

            def pair(i, windows=False, last=False, sums_of=None, first=False, part=None):
                step = chain(i, S["pair"], PAIR_STEPS)
                ph, b, use, rounds, seq = sums_of or (0, 0, 0, [], 0)

                def hots(k):
                    if k < len(rounds):
                        round_onehots(ph, use, rounds[k], chain(seq + k, S["hots"], 1))

                def take(k):
                    if k < len(rounds):
                        take_sums(b + NB * ph + rounds[k][0], b + rounds[k][0], len(rounds[k]))

                ranks_a(i, step)
                onehot(i * 2 + 1, 1)
                if first:
                    places()
                hots(0)
                ranks_b(i, step)
                payload(i * 2, 0)
                if windows:
                    window_rest(i + WB0)
                if part is not None:
                    add_h_part(part)
                take(0)
                if len(rounds) == 3:
                    hots(1)
                if not last:
                    onehot(i * 2 + 2, 0)
                if windows:
                    window_low(i + WB0)
                if len(rounds) == 3:
                    take(1)
                hots(len(rounds) - 1 if len(rounds) > 1 else 9)
                payload(i * 2 + 1, 1)
                if len(rounds) > 1:
                    take(len(rounds) - 1)

            PAIRS1 = [[2 * r, 2 * r + 1] for r in range(R1)]
            PAIRS2 = [[2 * r, 2 * r + 1] for r in range(R2)]
            pair(0, windows=True, first=True)
            pair(1, windows=True)
            with dve.Fori(2, P2) as i:
                pair(i, windows=True)
            dve.wait_ge(S["const"], 3)
            link(V.reciprocal(rec_mark[:], rec_mark[:]))
            check_ranks(0)
            pair(P2, windows=True)
            with dve.Fori(P2 + 1, WP) as i:
                pair(i, windows=True)
            for i in range(WP, Q1):
                pair(i, part=i - WP)
            with dve.Fori(Q1, P3) as i:
                pair(i, sums_of=(0, (i - Q1) * S1, i - Q1 + 1, PAIRS1, (i - Q1) * R1))
            check_ranks(1)
            pair(P3, sums_of=(0, S1 * N1, N1 + 1, [[0]], N1 * R1))
            q = N1 * R1 + 1
            with dve.Fori(P3 + 1, NP - 1) as i:
                pair(i, sums_of=(1, (i - P3 - 1) * S2, i - P3, PAIRS2, (i - P3 - 1) * R2 + q))
            pair(NP - 1, last=True, sums_of=(1, (N2 - 1) * S2, N2, PAIRS2, (N2 - 1) * R2 + q))
            q += N2 * R2
            round_onehots(1, N2 + 1, [0], chain(q, S["hots"], 1))
            take_sums(NB + S2 * N2, S2 * N2, 1)
            q += 1
            check_ranks(2)

            one = [0]

            def tail_step(ins):
                one[0] += 1
                ins.then_inc(S["tail"], 1)
                dve.wait_ge(S["tail"], one[0])

            tail_step(V.tensor_scalar(bad[:, 0:1], bad[:, 0:1], 127.5, None, ALU.is_gt))
            tail_step(V.tensor_reduce(bad[:, 4:5], bad[:, 0:4], axis=AX.X, op=ALU.max))
            tail_step(V.tensor_copy(flag[:], bad[:, 4:5]))

            rounds_of = [[(b0 + k, min(2, n - k)) for k in range(0, n, 2)] for b0, n in batches]
            taken = [0]

            def tail_onehots(j):
                for b, m in rounds_of[j]:
                    taken[0] += 1
                    dve.wait_ge(S["tmark"], taken[0])
                    onehots_of(2, b % 8, m, b % TB)

            def means(j, total, q):
                n = batches[j][1]
                if total.shape[-1] == AW:
                    tail_step(V.tensor_scalar(cnt[:, 0, 0:n], total[:, :, MARK], rec_mark[0:BN, :], MAGIC, ALU.mult, ALU.add))
                    tail_step(V.tensor_reduce(mean[:, 0:n, :], total[:, :, 0:3 * D].rearrange("p v (c f) -> p v f c", c=3), axis=AX.X, op=ALU.add))
                    part = mean[:, 0:n, :]
                else:
                    tail_step(V.tensor_scalar(cnt[:, 0, 0:n], total[:, :, D], rec_mark[0:BN, :], MAGIC, ALU.mult, ALU.add))
                    part = total[:, :, 0:D]
                tail_step(V.tensor_scalar(cnt[:, 1, 0:n], cnt[:, 0, 0:n], -MAGIC, 1.0, ALU.add, ALU.max))
                tail_step(V.reciprocal(cnt[:, 2, 0:n], cnt[:, 1, 0:n]))
                if j >= 2:
                    dve.wait_ge(q["catT"], j - 1)
                V.tensor_tensor(cat[:, j % 2, 0:n, D:2 * D], part, cnt[:, 2, 0:n].unsqueeze(2).to_broadcast((BN, n, D)),
                                ALU.mult).then_inc(q["cat"], 1)

            def take_tail(j):
                b0, n = batches[j]
                dve.wait_ge(S["ag"], 2 * NB + b0 + n)
                k0 = 4 + j % 2 * 2
                means(j, bank[0:BN, k0:k0 + 2, :].rearrange("p k (v w) -> p (k v) w", w=256)[:, 0:n, 0:AW], NODE)

            def node(j, q):
                b0, n = batches[j]
                dve.wait_ge(q["o"], j + 1)
                V.tensor_tensor(ot[:, b0:b0 + n, :], bank[0:BN, 2 + j % 2, 0:n * D].rearrange("p (v f) -> p v f", f=D),
                                xs[:, b0:b0 + n, :], ALU.add).then_inc(q["oe"], 1)

            tail_onehots(0)
            for j in range(NJ):
                if j + 1 < NJ:
                    tail_onehots(j + 1)
                if j >= 3:
                    node(j - 3, NODE)
                take_tail(j)
            node(NJ - 3, NODE)
            node(NJ - 2, NODE)
            node(NJ - 1, NODE)
            dve.wait_ge(S["oe"], NJ)
            dve.sem_inc(S["flag"], 1)
            dve.wait_ge(S["flag"], 1)
            is_bad = dve.value_load(flag[0:1, 0:1], min_val=0, max_val=1)
            with dve.If(is_bad > 0):
                dve.wait_ge(L["dT"], 1)
                V.tensor_copy(dstL.rearrange("p g k -> p k g"), bank[:, 0, 0:K * NG].rearrange("p (k g) -> p k g", g=NG)).then_inc(L["dTe"], 1)
                for b in range(NB):
                    dve.wait_ge(L["pj"], b + 1)
                    if b >= 2:
                        dve.wait_ge(l_pst[b % 2], 16 * (b // 2))
                    V.tensor_copy(s_proj[:, b % 2, :], bank[0:BN, b % 2, 0:HID]).then_inc(L["pje"], 1)
                dve.wait_ge(L["iota"], 1)
                dve.wait_ge(L["dTe"], 1)

                def group(g, first):
                    if not first:
                        for k in range(K):
                            dve.wait_ge(l_g[k], g * 16)
                    V.tensor_copy(dst_now, dstL[:, bass.ds(g, 1), :].rearrange("p a k -> p (a k)")).then_inc(L["stage"], 1)
                    for k in range(K):
                        dve.wait_ge(L["eT"], g * K + k + 1)
                        V.tensor_copy(s_eaT, bank[0:D, 0, 0:128]).then_inc(L["eTe"], 1)
                        if k or not first:
                            dve.wait_ge(L["used"], g * K + k)
                        V.tensor_scalar(s_onehot.rearrange("p b n -> p (b n)"), node_row,
                                        srcL[:, bass.ds(g, 1), k], None, ALU.is_equal)
                        V.tensor_copy(s_msg[:, D:D + 1], mark[:, bass.ds(g, 1), k])
                        dve.wait_ge(L["M"], g * K + k + 1)
                        V.tensor_tensor(s_msg[:, 0:D], bank[:, 2, 0:D], b1b_all[:], ALU.add).then_inc(L["Me"], 1)

                group(0, True)
                with dve.Fori(1, NG) as g:
                    group(g, False)
                dve.wait_ge(L["used"], NG * K)
                for b in range(NB):
                    last = V.tensor_copy(sums[:, b, :], slow_acc(b))
                last.then_inc(L["Me"], 1)
                dve.wait_ge(L["Me"], NG * K + 1)
                for j, (b0, n) in enumerate(batches):
                    means(j, sums[:, b0:b0 + n, :], AGAIN)
                    node(j, AGAIN)
            dve.sem_inc(S["gate"], 1)

        @block.scalar
        def _(act):
            A = nc.scalar
            act.wait_ge(S["zero"], 1)
            A.activation(warm[:], zeros[0:1, 0:1], ACT.Sqrt)

            def squares(part):
                b0, b1 = PARTS[part]
                act.wait_ge(S["xc"], part + 1)
                A.activation(ot[:, b0:b1, :], xc[:, b0:b1, :], ACT.Square).then_inc(S["sq"], 1)
                act.wait_ge(S["sq"], part + 1)
                A.activation(xc[:, b0:b1, :], xc[:, b0:b1, :], ACT.Relu).then_inc(S["rx"], 1)

            def deviation(part):
                b0, b1 = PARTS[part]
                act.wait_ge(S["var"], part + 1)
                A.activation(stat[:, 2, b0:b1], stat[:, 1, b0:b1], ACT.Sqrt).then_inc(S["sd"], 1)

            def evacuate_hT(j):
                b0, n = batches[j]
                act.wait_ge(S["hTt"], j + 1)
                A.copy(hT[:, b0 * BN:(b0 + n) * BN], bank[0:D, hT_bank(j), 0:n * BN]).then_inc(S["hTa"], 1)

            squares(0)
            deviation(0)
            act.wait_ge(S["setT"], 1)
            A.copy(w1aT[:], bank[:, 0, 0:HID])
            A.copy(we2T[D:2 * D, :], bank[D:2 * D, 0, 0:HID])
            A.copy(we2T[0:D, :], bank[0:D, 0, 128:128 + HID])
            A.copy(w1bT[:], bank[:, 0, 256:256 + D])
            A.copy(w2aT[:], bank[:, 0, 384:384 + HID])
            A.copy(wrzT[:], bank[0:D, 1, 128:128 + D])
            A.copy(wrhT[:], bank[0:D, 1, 256:256 + D]).then_inc(S["setE"], 1)
            evacuate_hT(0)
            act.wait_ge(S["hTa"], 1)
            act.wait_ge(S["hTd"], 1)

            def take_hT(j):
                if not isinstance(j, int) or j:
                    act.wait_ge(S["proj"], j)
                A.copy(hTw[:], hT[:, bass.ds(j * (4 * WS), WC)]).then_inc(S["hw"], 1)

            def window_high(j):
                act.wait_ge(S["proj"], j + 1)
                A.copy(pwin[:, bass.ds(j * 4, 4), 0, :], bank[:, SPARE, :].rearrange("p (w h) -> p w h", h=HID)).then_inc(S["phi"], 1)

            def window_middle(j):
                act.wait_ge(S["pr1"], j + 1)
                A.copy(pwin[:, bass.ds(j * 4, 4), 1, :], rest[:].rearrange("p (w h) -> p w h", h=HID)).then_inc(S["pmid"], 1)

            def evacuate(g, u):
                act.wait_ge(S["T"], g + 1)
                if not isinstance(g, int) or g >= 2:
                    act.wait_ge(S["H"], (g - 1) * 2)
                A.copy(eaT[:, u, :], pT).then_inc(S["Te"], 1)

            for j in range(WB0):
                take_hT(j)
                window_high(j)
                if j == 1:
                    deviation(1)
                if j == 0:
                    squares(1)
                    act.wait_ge(S["setW"], 1)
                    A.copy(w2r[:], bank[:, 1, 0:D])
                    A.copy(bias_row[:], bank[0:1, 1, 128:128 + D]).then_inc(S["setWe"], 1)
                else:
                    evacuate(0, 0)
                window_middle(j)

            def group(g, u, i, first, last, windows):
                if windows and u == 0:
                    take_hT(i + WB0)
                if not last:
                    evacuate(g + 1, 1 - u)
                for par in range(2):
                    act.wait_ge(S["H"], g * 2 + par + 1)
                    if not (first and u == 0):
                        act.wait_ge(S["M"], g * 2 + par - 1)
                    A.activation(rT[:, par, :], pH[:, par, :], ACT.Relu, bias=b1a_col[:]).then_inc(S["rl"], 1)
                if is_early(i) and (u == 0 or i == 1):
                    evacuate_hT(2 + 2 * i + 2 * u)
                act.wait_ge(S["M"], g * 2 + 2)
                if not first:
                    act.wait_ge(s_sc[u], i * (16 * K))
                A.copy(pay[:, u, :, HIGH:HIGH + D], pM.rearrange("p (k f) -> p k f", f=D)).then_inc(S["hi"], 1)
                if is_early(i) and u == 0:
                    evacuate_hT(3 + 2 * i)
                act.wait_ge(S["r1"], g + 1)
                A.copy(pay[:, u, :, MID:MID + D], r1[:, u, :, :]).then_inc(S["mid"], 1)
                if windows and u == 0:
                    window_high(i + WB0)
                    window_middle(i + WB0)
                if u and isinstance(i, int) and i == 1:
                    act.wait_ge(S["hTa"], NJ - 1)
                    act.wait_ge(S["const"], 1)

            def pair(i, first=False, last=False, windows=False):
                group(i * 2, 0, i, first, False, windows)
                group(i * 2 + 1, 1, i, first, last, windows)

            act.wait_ge(S["const"], 2)
            act.wait_ge(S["w_in"], 16 * NWT)
            pair(0, first=True, windows=True)
            pair(1, windows=True)
            with act.Fori(2, WP) as i:
                pair(i, windows=True)
            with act.Fori(WP, NP - 1) as i:
                pair(i)
            pair(NP - 1, last=True)

            def node(j, q):
                b0, n = batches[j]
                act.wait_ge(q["catT"], j + 1)
                A.copy(catT[D:2 * D, b0 * BN:(b0 + n) * BN], bank[D:2 * D, 0, 0:n * BN]).then_inc(q["catE"], 1)
                act.wait_ge(q["z1"], j + 1)
                A.activation(z1T[:, 0:n * BN], bank[:, 1, 0:n * BN], ACT.Relu, bias=b2a_col[:]).then_inc(q["z1e"], 1)

            def tail_marks(j):
                b0, n = batches[j]
                for k in range(0, n, 2):
                    m, v0 = min(2, n - k), (b0 + k) % TB
                    for v in range(v0, v0 + m):
                        act.wait_ge(s_row[v], 16 * (USES[2][v] + (b0 + k) // TB + 1))
                    A.copy(rmark[:, v0 * C[2]:(v0 + m) * C[2]], rows[:, v0 * C[2]:(v0 + m) * C[2], MARK]).then_inc(S["tmark"], 1)

            tail_marks(0)
            tail_marks(1)
            tail_marks(2)
            for j in range(NJ):
                if j + 3 < NJ:
                    tail_marks(j + 3)
                node(j, NODE)
            act.wait_ge(S["flag"], 1)
            is_bad = act.value_load(flag[0:1, 0:1], min_val=0, max_val=1)
            with act.If(is_bad > 0):
                with act.Fori(0, NG) as g:
                    for k in range(K):
                        act.wait_ge(L["H"], g * K + k + 1)
                        A.activation(s_rT, bank[:, 1, 0:128], ACT.Relu, bias=b1a_col[:]).then_inc(L["r"], 1)
                for j in range(NJ):
                    node(j, AGAIN)
            act.sem_inc(S["gate"], 1)

        @block.tensor
        def _(pe):
            T = nc.tensor
            pe.wait_ge(S["w_in"], 16 * NWT)
            pe.wait_ge(S["id"], 2)
            I = ident
            T.transpose(bank[:, 0, 0:HID], w1a_in[:], I[:])
            T.transpose(bank[0:D, 0, 128:128 + HID], w1a_in[:, D:2 * D], I[:])
            T.transpose(bank[:, 0, 256:256 + D], w1b_in[:], I[0:D, 0:D])
            T.transpose(bank[:, 0, 384:384 + HID], w2a_in[:], I[:])
            T.transpose(bank[0:D, 1, 128:128 + D], wr_in[:, 0:D], I[0:D, 0:D])
            T.transpose(bank[0:D, 1, 256:256 + D], wr_in[:, D:2 * D], I[0:D, 0:D]).then_inc(S["setT"], 1)
            pe.wait_ge(S["fsrc"], 1)
            for k in range(K):
                T.transpose(bank[:, 2, k * NG:(k + 1) * NG], idx_f[:].rearrange("g (p k) -> g k p", k=K)[:, k, :], I[0:NG, 0:NG])
            pe.wait_ge(S["h"], 1)

            def transpose_h(j):
                b0, n = batches[j]
                if j >= 2 and j % 2 == 0:
                    pe.wait_ge(S["pr1"], j // 2 + 1)
                elif j >= 3:
                    pe.wait_ge(S["hTa"], j - 1)
                for v in range(n):
                    last = T.transpose(bank[0:D, hT_bank(j), v * BN:(v + 1) * BN], h[:, b0 + v, :], I[0:BN, 0:BN])
                last.then_inc(S["hTt"], 1)

            for j in range(2):
                transpose_h(j)
            pe.wait_ge(S["wready"], 1)
            T.transpose(bank[0:1, 3, 0:NG], wstat[:, 2:3], I[0:NG, 0:NG])
            T.transpose(bank[0:1, 3, 128:128 + NG], wstat[:, 3:4], I[0:NG, 0:NG]).then_inc(S["setT"], 1)
            pe.wait_ge(S["setE"], 1)

            def make_windows(j, summed=None):
                pe.wait_ge(S["hw"], j + 1)
                if not isinstance(j, int) or j:
                    pe.wait_ge(S["pr1"], j)
                for v in range(4):
                    last = T.matmul(bank[:, SPARE, v * 128:(v + 1) * 128], hTw[:, v * WS:v * WS + 128], w1aT[0:D, :],
                                    start=(v == 0), stop=True, skip_group_check=True)
                last.then_inc(S["proj"], 1)

            def spread(g, u, load_count):
                pe.wait_ge(s_ea[u], load_count)
                if not isinstance(g, int) or g >= 1:
                    pe.wait_ge(S["Te"], g)
                pe.sem_inc(S["gate"], 1)
                for j in range(4):
                    last = T.transpose(pT[:, j * 128:(j + 1) * 128], ea[:, u, 2 * j:2 * j + 2, :].rearrange("p k f -> p (k f)"), I[:])
                last.then_inc(S["T"], 1)
                if not isinstance(g, int) or g >= 1:
                    pe.wait_ge(S["oh"], g)
                for par in range(2):
                    last = T.matmul(pR[:, par, :], ident_b[:, bass.ds(g, 1)].to_broadcast((128, 128)),
                                    rel[:, par, :, :].rearrange("p j e -> p (j e)"), start=True, stop=True)
                last.then_inc(S["Rb"], 1)

            make_windows(0)
            T.matmul(bank[:, 1, 0:D], w2b_in[:], wrzT[:], start=True, stop=True)
            T.matmul(bank[0:1, 1, 128:128 + D], b2b_col[:], wrzT[:], start=True, stop=False)
            T.matmul(bank[0:1, 1, 128:128 + D], I[0:1, 0:1], br_row[:], start=False, stop=True).then_inc(S["setW"], 1)
            pe.wait_ge(S["const"], 2)
            pe.wait_ge(S["srcE"], 1)
            spread(0, 0, 16)
            make_windows(1)
            pe.wait_ge(S["setWe"], 1)

            def ranks_from(ph):
                if ph:
                    pe.wait_ge(S["rkf"], ph)
                T.matmul(RANK, ones_row[:], base[:, ph, :], start=True, stop=True, skip_group_check=True)

            def group(g, u, i, first, nxt, windows, new_phase=0):
                w = pe.value_load(win[0:1, bass.ds(g, 1)], min_val=0, max_val=NWIN - 1)
                if nxt is not None:
                    spread(g + 1, 1 - u, nxt)
                for par in range(2):
                    if par == 0:
                        if windows and u == 0:
                            pe.wait_ge(S["plo"], i + WB0)
                        pe.wait_ge(S["Te"], g + 1)
                        pe.wait_ge(S["oh"], g + 1)
                    if not first:
                        pe.wait_ge(S["rl"], g * 2 + par - 1)
                    T.matmul(pH[:, par, :], we2T[par * D:(par + 1) * D, :], eaT[par * D:(par + 1) * D, u, :], start=True, stop=False)
                    for c in range(3):
                        last = T.matmul(pH[:, par, :], pwin[:, bass.ds(w, 1), c, :].rearrange("p a h -> p (a h)"), oh[:, u, par, :],
                                        start=False, stop=(c == 2))
                    last.then_inc(S["H"], 1)
                if u == 0:
                    if new_phase:
                        ranks_from(new_phase)
                    pe.wait_ge(S["rc"], i + 1)
                    T.matmul(RANK, below[:], rowcnt[:], start=False, stop=True, skip_group_check=True).then_inc(S["rk"], 1)
                else:
                    pe.wait_ge(S["pair"], i * PAIR_STEPS + 3)
                    T.matmul(RANK, not_below[:], rowcnt[:], start=False, stop=True, skip_group_check=True).then_inc(S["rkd"], 1)

            def messages(g, first):
                if not first:
                    pe.wait_ge(S["r1"], g)
                else:
                    pe.wait_ge(S["srcE"], 2)
                T.matmul(pM, ones_b[:], b1b_rows[:].rearrange("p k f -> p (k f)"), start=True, stop=False, skip_group_check=True)
                for par in range(2):
                    pe.wait_ge(S["rl"], g * 2 + par + 1)
                    for j in range(4):
                        k = 2 * j + par
                        last = T.matmul(pM[:, k * D:(k + 1) * D], rT[:, par, j * 128:(j + 1) * 128], w1bT[:],
                                        start=False, stop=True, skip_group_check=True)
                    last.then_inc(S["M"], 1)

            def sum_blocks(ph, n, b, v, m, r, rounds, to=SPARE):
                if rounds is not None:
                    pe.wait_ge(S["ae"], rounds)
                pe.wait_ge(S["oh2"], n + m)
                for a in range(m):
                    hot, tiles = one_hot_rows(ph, v + a), row_tiles(ph, r + a)
                    for t in range(C[ph]):
                        last = T.matmul(acc(a, to), hot[:, 0, :, t], tiles[:, t, 0:AW], start=(t == 0), stop=(t == C[ph] - 1), skip_group_check=True)
                    if ph:
                        last = T.matmul(acc(a, to)[:, HIGH:AW], I[0:BN, 0:BN], sums[:, bass.ds(b + a, 1), :].rearrange("p a f -> p (a f)"),
                                        start=False, stop=True, skip_group_check=True)
                    last.then_inc(S["ag"], 1)

            def h_part(a):
                if a:
                    pe.wait_ge(S["xhe"], a)
                for n, b in enumerate(range(h_parts[a][0], sum(h_parts[a]))):
                    o_b = bank[0:BN, SPARE, n * D:(n + 1) * D]
                    T.matmul(o_b, hT[:, b * BN:(b + 1) * BN], wrhT[:], start=(n == 0), stop=False, skip_group_check=True)
                    last = T.matmul(o_b, ones_row[:, 0:BN], bias_row[:], start=False, stop=True, skip_group_check=True)
                last.then_inc(S["xh"], 1)

            def pair(i, first=False, last=False, windows=False, sums_of=None, part=None, new_phase=0):
                ph, b, rounds, seq = sums_of or (0, 0, [], 0)

                def sum_round(k):
                    if k < len(rounds):
                        vs = rounds[k]
                        so_far = None if seq is None and k == 0 else (0 if seq is None else seq) + k
                        sum_blocks(ph, b + NB * ph + vs[0], b + vs[0], vs[0], len(vs), vs[0], so_far)

                group(i * 2, 0, i, first, i * 16 + 16 if not last else 16 * (NP + 1), windows, new_phase)
                if is_early(i):
                    pe.wait_ge(S["h"], 2)
                    transpose_h(2 + 2 * i)
                messages(i * 2, first)
                if is_early(i):
                    transpose_h(3 + 2 * i)
                    pe.wait_ge(S["hTa"], 3 + 2 * i)
                if windows:
                    make_windows(i + WB0)
                if part is not None:
                    h_part(part)
                sum_round(0)
                group(i * 2 + 1, 1, i, False, None if last else i * 16 + 32, windows)
                if len(rounds) == 3:
                    sum_round(1)
                if isinstance(i, int) and i == 1:
                    transpose_h(6)
                messages(i * 2 + 1, False)
                if len(rounds) > 1:
                    sum_round(len(rounds) - 1)

            PAIRS1 = [[2 * r, 2 * r + 1] for r in range(R1)]
            PAIRS2 = [[2 * r, 2 * r + 1] for r in range(R2)]
            ranks_from(0)
            pair(0, first=True, windows=True)
            pair(1, windows=True)
            with pe.Fori(2, P2) as i:
                pair(i, windows=True)
            pair(P2, windows=True, new_phase=1)
            with pe.Fori(P2 + 1, WP) as i:
                pair(i, windows=True)
            pe.wait_ge(S["plo"], NWB)
            for i in range(WP, Q1):
                pair(i, part=i - WP)
            pe.wait_ge(S["xhe"], len(h_parts))
            pair(Q1, sums_of=(0, 0, PAIRS1, None))
            with pe.Fori(Q1 + 1, P3) as i:
                pair(i, sums_of=(0, (i - Q1) * S1, PAIRS1, (i - Q1) * R1))
            pair(P3, sums_of=(0, S1 * N1, [[0]], N1 * R1), new_phase=2)
            q = N1 * R1 + 1
            with pe.Fori(P3 + 1, NP - 1) as i:
                pair(i, sums_of=(1, (i - P3 - 1) * S2, PAIRS2, (i - P3 - 1) * R2 + q))
            pair(NP - 1, last=True, sums_of=(1, (N2 - 1) * S2, PAIRS2, (N2 - 1) * R2 + q))
            q += N2 * R2
            sum_blocks(1, NB + S2 * N2, S2 * N2, 0, 1, 0, q)
            q += 1

            def transposes(j, q):
                b0, n = batches[j]
                pe.wait_ge(q["cat"], j + 1)
                if j:
                    pe.wait_ge(q["catE"], j)
                for v in range(n):
                    last = T.transpose(bank[:, 0, v * BN:(v + 1) * BN], cat[:, j % 2, v, :], I[0:BN, 0:BN])
                last.then_inc(q["catT"], 1)

            def z1(j, q):
                b0, n = batches[j]
                c = n * BN
                pe.wait_ge(q["catE"], j + 1)
                T.matmul(bank[:, 1, 0:c], w2aT[:], catT[:, b0 * BN:b0 * BN + c], start=True, stop=True).then_inc(q["z1"], 1)

            def outs(j, q):
                b0, n = batches[j]
                pe.wait_ge(q["z1e"], j + 1)
                if j >= 2:
                    pe.wait_ge(q["oe"], j - 1)
                for v in range(n):
                    last = T.matmul(bank[0:BN, 2 + j % 2, v * D:(v + 1) * D], z1T[:, v * BN:(v + 1) * BN], w2r[:],
                                    start=(v == 0), stop=True, skip_group_check=True)
                last.then_inc(q["o"], 1)

            def tail_sums(j, k):
                b0, n = batches[j]
                if j < 2:
                    if j and k == 0:
                        pe.wait_ge(S["ae"], q)
                        pe.wait_ge(S["rkf"], 3)
                elif k == 0:
                    pe.wait_ge(S["cat"], j - 1)
                sum_blocks(2, 2 * NB + b0 + k, b0 + k, b0 % 8 + k, min(2, n - k), b0 % TB + k, None, to=4 + j % 2 * 2 + k // 2)

            for j in range(NJ + 2):
                if j < NJ:
                    for k in range(0, batches[j][1], 2):
                        tail_sums(j, k)
                if j >= 2:
                    z1(j - 2, NODE)
                if 1 <= j <= NJ:
                    transposes(j - 1, NODE)
                if j >= 2:
                    outs(j - 2, NODE)

            pe.wait_ge(S["flag"], 1)
            is_bad = pe.value_load(flag[0:1, 0:1], min_val=0, max_val=1)
            with pe.If(is_bad > 0):
                pe.wait_ge(S["fdst"], 1)
                for k in range(K):
                    last = T.transpose(bank[:, 0, k * NG:(k + 1) * NG], idx_f[:].rearrange("g (p k) -> g k p", k=K)[:, k, :], I[0:NG, 0:NG])
                last.then_inc(L["dT"], 1)
                pe.wait_ge(L["dTe"], 1)
                for b in range(NB):
                    if b >= 2:
                        pe.wait_ge(L["pje"], b - 1)
                    T.matmul(bank[0:BN, b % 2, 0:HID], hT[:, b * BN:(b + 1) * BN], w1aT[0:D, :], start=True, stop=True).then_inc(L["pj"], 1)
                pe.wait_ge(L["pje"], NB)

                def slow_group(g, u, loads, first):
                    pe.wait_ge(l_ea[u], loads)
                    pe.sem_inc(S["gate"], 1)
                    for k in range(K):
                        t = g * K + k
                        T.transpose(bank[0:D, 0, 0:128], ea[:, u, k, :], I[:]).then_inc(L["eT"], 1)
                        pe.wait_ge(l_g[k], g * 16 + 16)
                        T.matmul(bank[:, 1, 0:128], pg[:, k, :], I[:], start=True, stop=False)
                        pe.wait_ge(L["eTe"], t + 1)
                        T.matmul(bank[:, 1, 0:128], we2T[0:D, :], s_eaT, start=False, stop=True).then_inc(L["H"], 1)
                        pe.wait_ge(L["r"], t + 1)
                        T.matmul(bank[:, 2, 0:D], s_rT, w1bT[:], start=True, stop=True).then_inc(L["M"], 1)
                        pe.wait_ge(L["Me"], t + 1)
                        for b in range(NB):
                            last = T.matmul(slow_acc(b), s_onehot[:, b, :], s_msg[:], start=(first and k == 0 and b % PER_BANK == 0),
                                            stop=False, skip_group_check=True)
                        last.then_inc(L["used"], 1)

                slow_group(0, 0, 16, True)
                slow_group(1, 1, 16, False)
                with pe.Fori(1, NP - 1) as i:
                    slow_group(i * 2, 0, i * 16 + 16, False)
                    slow_group(i * 2 + 1, 1, i * 16 + 16, False)
                slow_group(NG - 2, 0, 16 * NP, False)
                slow_group(NG - 1, 1, 16 * (NP + 1), False)
                for j in range(NJ):
                    transposes(j, AGAIN)
                    z1(j, AGAIN)
                    outs(j, AGAIN)
            pe.sem_inc(S["gate"], 1)


_INS = ['x', 'src', 'dst', 'edge_attr_64'] + ['L0_gnn_' + w for w in ('W1a', 'b1a', 'W1b', 'b1b', 'W2a', 'b2a', 'W2b', 'b2b', 'Wr', 'br')]


def kernel(**inputs):
    import numpy as np
    import concourse.bacc as bacc
    from concourse.bass_utils import run_bass_kernel_spmd
    nc = bacc.Bacc("TRN2", target_bir_lowering=False, num_devices=1)
    arrays, args = {}, []
    for name in _INS:
        a = np.ascontiguousarray(inputs[name])
        arrays[f"in_{name}"] = a
        args.append(nc.dram_tensor(f"in_{name}", a.shape, mybir.dt.from_np(a.dtype), kind="ExternalInput").ap())
    args.append(nc.dram_tensor("out_0", inputs['x'].shape, mybir.dt.float32, kind="ExternalOutput").ap())
    gnn_layer(nc, *args)
    r = run_bass_kernel_spmd(nc, [arrays], core_ids=[0])
    return r.results[0]["out_0"]
```
